# Optimizing a Trainium2 kernel written in Bass

```python
import numpy as np
import jax
import jax.numpy as jnp

def _softmax(x, axis=-1):
    return jax.nn.softmax(x, axis=axis)

def _gelu(x):
    return jax.nn.gelu(x, approximate=True)

def _silu(x):
    return jax.nn.silu(x)

def _sigmoid(x):
    return jax.nn.sigmoid(x)

def _layernorm(x, axis=-1, eps=1e-05):
    m = jnp.mean(x, axis=axis, keepdims=True)
    v = jnp.var(x, axis=axis, keepdims=True)
    return (x - m) / jnp.sqrt(v + eps)

def _scatter_add(tgt, idx, src, axis=0):
    return tgt.at[idx].add(src)

def _segment_sum(src, seg, n):
    return jax.ops.segment_sum(src, seg, n)
kernel_name = 'mk_decoder_preln_d1_seqx_r4_e17f54'

def setup_inputs(seed: int=0):
    np.random.seed(seed)
    _w = jnp.asarray

    def _rec_inputs():
        import jax
        import jax.numpy as jnp
        _rk = jax.random.key(seed)
        x = -7.109e-05 + 0.9999 * jax.random.normal(jax.random.fold_in(_rk, 1), (4, 512, 512), jnp.float32)
        _lenS = 512 - jax.random.randint(jax.random.fold_in(_rk, 7), (4,), 0, max(1, 512 // 4) + 1, jnp.int32)
        _lenS2 = 512 - jax.random.randint(jax.random.fold_in(_rk, 8), (4,), 0, max(1, 512 // 4) + 1, jnp.int32)
        _ctx_2048P = jax.random.normal(jax.random.fold_in(_rk, 11), (4, 16, 512), jnp.float32)
        _ctx_2048c = jax.random.dirichlet(jax.random.fold_in(_rk, 511), 0.3 * jnp.ones((16,), jnp.float32), (4, 512))
        _ctx_2048t = jnp.einsum('bsk,bkd->bsd', _ctx_2048c, _ctx_2048P)
        _ctx_2048t = _ctx_2048t * jax.lax.rsqrt(jnp.mean(jnp.square(_ctx_2048t)) + 1e-12) * 0.953939
        ctx_2048 = -3.05549e-07 + 0.0199987 * (_ctx_2048t + 0.3 * jax.random.normal(jax.random.fold_in(_rk, 611), (4, 512, 512), jnp.float32))
        return (x, ctx_2048)
    x, ctx_2048 = _rec_inputs()

    def _L0_attn_setup():
        import jax, jax.numpy as jnp
        import numpy as np
        N_HEAD = 32
        N_KV_HEAD = 8
        HEAD_DIM = 64
        N_EMBD = 512
        B, T = (2, 512)
        ROPE_BASE = 10000.0

        def _rope_cos_sin(T, head_dim, dtype):
            pos = jnp.arange(T, dtype=jnp.float32)
            dim_arr = jnp.arange(0, head_dim, 2, dtype=jnp.float32)
            freqs = ROPE_BASE ** (-dim_arr / head_dim)
            theta = jnp.outer(pos, freqs)
            cos = jnp.concatenate([jnp.cos(theta), jnp.cos(theta)], axis=-1)
            sin = jnp.concatenate([jnp.sin(theta), jnp.sin(theta)], axis=-1)
            return (cos[None, :, None, :].astype(dtype), sin[None, :, None, :].astype(dtype))

        def _rotate_half(v):
            h = v.shape[-1] // 2
            return jnp.concatenate([-v[..., h:], v[..., :h]], axis=-1)
        key = jax.random.key(seed)
        kx, kq, kk, kv, ko = jax.random.split(key, 5)
        s = 1.0 / np.sqrt(N_EMBD)
        return {'x': jax.random.normal(kx, (B, T, N_EMBD), dtype=jnp.float32), 'wq': jax.random.normal(kq, (N_EMBD, N_HEAD * HEAD_DIM), dtype=jnp.float32) * s, 'wk': jax.random.normal(kk, (N_EMBD, N_KV_HEAD * HEAD_DIM), dtype=jnp.float32) * s, 'wv': jax.random.normal(kv, (N_EMBD, N_KV_HEAD * HEAD_DIM), dtype=jnp.float32) * s, 'wo': jax.random.normal(ko, (N_HEAD * HEAD_DIM, N_EMBD), dtype=jnp.float32) * s}
    _L0_attn_all = _L0_attn_setup()
    _L0_attn_in = {k: v for k, v in _L0_attn_all.items() if k in ('wq', 'wk', 'wv', 'wo')}
    del _L0_attn_all

    def _L0_xattn_setup():
        import jax, jax.numpy as jnp
        import numpy as np
        FP8_MAX = 448.0
        ACT_EPS = 0.0001
        W_EPS = 1e-06
        BLK = 128

        def quant_dequant_act_1x128(x):
            E, M, K = x.shape
            xb = x.reshape(E, M, K // BLK, BLK)
            amax = jnp.max(jnp.abs(xb), axis=-1, keepdims=True)
            safe = jnp.maximum(amax, ACT_EPS)
            q = (xb * (FP8_MAX / safe)).astype(jnp.float8_e4m3fn)
            return (q.astype(jnp.float32) * (safe / FP8_MAX)).reshape(E, M, K)

        def quant_dequant_weight_128x128(w):
            E, N, K = w.shape
            wb = w.reshape(E, N // BLK, BLK, K // BLK, BLK)
            amax = jnp.max(jnp.abs(wb), axis=(2, 4), keepdims=True)
            safe = jnp.maximum(amax, W_EPS)
            q = (wb * (FP8_MAX / safe)).astype(jnp.float8_e4m3fn)
            return (q.astype(jnp.float32) * (safe / FP8_MAX)).reshape(E, N, K)
        key = jax.random.key(seed)
        kx, kw = jax.random.split(key)
        E, M, K, N = (8, 1024, 512, 512)
        x = jax.random.normal(kx, (E, M, K), dtype=jnp.float32)
        weight = jax.random.normal(kw, (E, N, K), dtype=jnp.float32) * 0.02
        return {'x': x, 'weight': weight}
    _L0_xattn_all = _L0_xattn_setup()
    _L0_xattn_in = {k: v for k, v in _L0_xattn_all.items() if k in ()}
    del _L0_xattn_all

    def _L0_ffn_setup():
        import jax, jax.numpy as jnp
        import numpy as np
        B, S, D = (4, 512, 512)
        E = 8
        H = 704
        CAP_F = 1.0

        def _moe(x, Wg, W1, W3, W2, sw1, sw3, sw2):
            b, sl, d = x.shape
            T = b * sl
            C = int(CAP_F * T / E)
            xt = x.reshape(T, d)
            probs = jax.nn.softmax(xt @ Wg, axis=-1)
            eidx = jnp.argmax(probs, axis=-1)
            gate = jnp.take_along_axis(probs, eidx[:, None], 1)[:, 0]
            oh = jax.nn.one_hot(eidx, E, dtype=jnp.int32)
            pos = (jnp.cumsum(oh, axis=0) * oh).sum(-1) - 1
            keep = pos < C
            flat = jnp.where(keep, eidx * C + pos, E * C)
            xd = jnp.zeros((E * C, d), x.dtype).at[flat].set(xt, mode='drop')
            xd = xd.reshape(E, C, d)
            h = jax.nn.silu(jnp.einsum('ecd,edh->ech', xd, W1)) * jnp.einsum('ecd,edh->ech', xd, W3)
            oe = jnp.einsum('ech,ehd->ecd', h, W2).reshape(E * C, d)
            out = jnp.take(oe, jnp.minimum(flat, E * C - 1), axis=0)
            out = out * (gate * keep.astype(x.dtype))[:, None]
            shared = jax.nn.silu(xt @ sw1) * (xt @ sw3) @ sw2
            return (out + shared).reshape(b, sl, d)
        key = jax.random.key(seed)
        ks = jax.random.split(key, 8)
        s = lambda fan: 1.0 / np.sqrt(fan)
        return {'x': jax.random.normal(ks[0], (B, S, D), jnp.float32), 'Wg': jax.random.normal(ks[1], (D, E), jnp.float32) * s(D), 'W1': jax.random.normal(ks[2], (E, D, H), jnp.float32) * s(D), 'W3': jax.random.normal(ks[3], (E, D, H), jnp.float32) * s(D), 'W2': jax.random.normal(ks[4], (E, H, D), jnp.float32) * s(H), 'sw1': jax.random.normal(ks[5], (D, H), jnp.float32) * s(D), 'sw3': jax.random.normal(ks[6], (D, H), jnp.float32) * s(D), 'sw2': jax.random.normal(ks[7], (H, D), jnp.float32) * s(H)}
    _L0_ffn_all = _L0_ffn_setup()
    _L0_ffn_in = {k: v for k, v in _L0_ffn_all.items() if k in ('Wg', 'W1', 'W3', 'W2', 'sw1', 'sw3', 'sw2')}
    del _L0_ffn_all
    return {'x': x, 'ctx_2048': ctx_2048, 'L0_attn_wq': _L0_attn_in['wq'], 'L0_attn_wk': _L0_attn_in['wk'], 'L0_attn_wv': _L0_attn_in['wv'], 'L0_attn_wo': _L0_attn_in['wo'], 'L0_ffn_Wg': _L0_ffn_in['Wg'], 'L0_ffn_W1': _L0_ffn_in['W1'], 'L0_ffn_W3': _L0_ffn_in['W3'], 'L0_ffn_W2': _L0_ffn_in['W2'], 'L0_ffn_sw1': _L0_ffn_in['sw1'], 'L0_ffn_sw3': _L0_ffn_in['sw3'], 'L0_ffn_sw2': _L0_ffn_in['sw2']}

def reference(x, ctx_2048, L0_attn_wq, L0_attn_wk, L0_attn_wv, L0_attn_wo, L0_ffn_Wg, L0_ffn_W1, L0_ffn_W3, L0_ffn_W2, L0_ffn_sw1, L0_ffn_sw3, L0_ffn_sw2):
    import jax
    import jax.numpy as jnp

    def _L0_attn_ref(x, wq, wk, wv, wo):
        import jax, jax.numpy as jnp
        import numpy as np
        N_HEAD = 32
        N_KV_HEAD = 8
        HEAD_DIM = 64
        N_EMBD = 512
        B, T = (2, 512)
        ROPE_BASE = 10000.0

        def _rope_cos_sin(T, head_dim, dtype):
            pos = jnp.arange(T, dtype=jnp.float32)
            dim_arr = jnp.arange(0, head_dim, 2, dtype=jnp.float32)
            freqs = ROPE_BASE ** (-dim_arr / head_dim)
            theta = jnp.outer(pos, freqs)
            cos = jnp.concatenate([jnp.cos(theta), jnp.cos(theta)], axis=-1)
            sin = jnp.concatenate([jnp.sin(theta), jnp.sin(theta)], axis=-1)
            return (cos[None, :, None, :].astype(dtype), sin[None, :, None, :].astype(dtype))

        def _rotate_half(v):
            h = v.shape[-1] // 2
            return jnp.concatenate([-v[..., h:], v[..., :h]], axis=-1)
        Bx, Tx, C = x.shape
        n_rep = N_HEAD // N_KV_HEAD
        xq = (x @ wq).reshape(Bx, Tx, N_HEAD, HEAD_DIM)
        xk = (x @ wk).reshape(Bx, Tx, N_KV_HEAD, HEAD_DIM)
        xv = (x @ wv).reshape(Bx, Tx, N_KV_HEAD, HEAD_DIM)
        cos, sin = _rope_cos_sin(Tx, HEAD_DIM, x.dtype)
        xq = xq * cos + _rotate_half(xq) * sin
        xk = xk * cos + _rotate_half(xk) * sin
        xk = jnp.repeat(xk, n_rep, axis=2)
        xv = jnp.repeat(xv, n_rep, axis=2)
        scale = 1.0 / np.sqrt(HEAD_DIM)
        scores = jnp.einsum('bqhd,bkhd->bhqk', xq, xk) * scale
        causal = jnp.tril(jnp.ones((Tx, Tx), dtype=bool))
        scores = jnp.where(causal[None, None], scores, -jnp.inf)
        probs = jax.nn.softmax(scores, axis=-1)
        out = jnp.einsum('bhqk,bkhd->bqhd', probs, xv).reshape(Bx, Tx, N_HEAD * HEAD_DIM)
        return out @ wo

    def _L0_xattn_ref(x, weight):
        import jax, jax.numpy as jnp
        import numpy as np
        FP8_MAX = 448.0
        ACT_EPS = 0.0001
        W_EPS = 1e-06
        BLK = 128

        def quant_dequant_act_1x128(x):
            E, M, K = x.shape
            xb = x.reshape(E, M, K // BLK, BLK)
            amax = jnp.max(jnp.abs(xb), axis=-1, keepdims=True)
            safe = jnp.maximum(amax, ACT_EPS)
            q = (xb * (FP8_MAX / safe)).astype(jnp.float8_e4m3fn)
            return (q.astype(jnp.float32) * (safe / FP8_MAX)).reshape(E, M, K)

        def quant_dequant_weight_128x128(w):
            E, N, K = w.shape
            wb = w.reshape(E, N // BLK, BLK, K // BLK, BLK)
            amax = jnp.max(jnp.abs(wb), axis=(2, 4), keepdims=True)
            safe = jnp.maximum(amax, W_EPS)
            q = (wb * (FP8_MAX / safe)).astype(jnp.float8_e4m3fn)
            return (q.astype(jnp.float32) * (safe / FP8_MAX)).reshape(E, N, K)
        xq = quant_dequant_act_1x128(x)
        wq = quant_dequant_weight_128x128(weight)
        return jnp.einsum('emk,enk->emn', xq, wq)

    def _L0_ffn_ref(x, Wg, W1, W3, W2, sw1, sw3, sw2):
        import jax, jax.numpy as jnp
        import numpy as np
        B, S, D = (4, 512, 512)
        E = 8
        H = 704
        CAP_F = 1.0

        def _moe(x, Wg, W1, W3, W2, sw1, sw3, sw2):
            b, sl, d = x.shape
            T = b * sl
            C = int(CAP_F * T / E)
            xt = x.reshape(T, d)
            probs = jax.nn.softmax(xt @ Wg, axis=-1)
            eidx = jnp.argmax(probs, axis=-1)
            gate = jnp.take_along_axis(probs, eidx[:, None], 1)[:, 0]
            oh = jax.nn.one_hot(eidx, E, dtype=jnp.int32)
            pos = (jnp.cumsum(oh, axis=0) * oh).sum(-1) - 1
            keep = pos < C
            flat = jnp.where(keep, eidx * C + pos, E * C)
            xd = jnp.zeros((E * C, d), x.dtype).at[flat].set(xt, mode='drop')
            xd = xd.reshape(E, C, d)
            h = jax.nn.silu(jnp.einsum('ecd,edh->ech', xd, W1)) * jnp.einsum('ecd,edh->ech', xd, W3)
            oe = jnp.einsum('ech,ehd->ecd', h, W2).reshape(E * C, d)
            out = jnp.take(oe, jnp.minimum(flat, E * C - 1), axis=0)
            out = out * (gate * keep.astype(x.dtype))[:, None]
            shared = jax.nn.silu(xt @ sw1) * (xt @ sw3) @ sw2
            return (out + shared).reshape(b, sl, d)
        return _moe(x, Wg, W1, W3, W2, sw1, sw3, sw2)
    x = x + _L0_attn_ref(_layernorm(x, axis=-1), L0_attn_wq, L0_attn_wk, L0_attn_wv, L0_attn_wo)
    x = x + _L0_xattn_ref(_layernorm(x, axis=-1), ctx_2048)
    x = x + _L0_ffn_ref(_layernorm(x, axis=-1), L0_ffn_Wg, L0_ffn_W1, L0_ffn_W3, L0_ffn_W2, L0_ffn_sw1, L0_ffn_sw3, L0_ffn_sw2)
    return x

_drawn_inputs = setup_inputs


def setup_inputs(seed=0):
    import zlib

    import numpy as np

    out = dict(_drawn_inputs(seed))
    spreads = {}
    factors = {}
    for name, (base, spread) in spreads.items():
        noise = np.random.default_rng([zlib.crc32(name.encode()), seed]).standard_normal(out[name].shape)
        drawn = base * np.exp(spread * noise) if base else spread * noise
        out[name] = jnp.asarray(drawn.astype(out[name].dtype))
    for name, factor in factors.items():
        out[name] = (out[name] * factor).astype(out[name].dtype)
    return out
```

```python
import numpy as np
import concourse.bass as bass
from concourse import mybir
from contextlib import ExitStack

NT, D, NB, TB = 16, 512, 4, 4
NG, HG, DH = 8, 4, 64
NE, CAP, HID = 8, 256, 704
EPS = 1e-5
BIG = 1e30


def later(fn):
    def make(*args, **kw):
        return lambda e: fn(e, *args, **kw)
    return make


do_activation = later(lambda e, *a, **k: e.activation(*a, **k))
do_bn_aggr = later(lambda e, *a, **k: e.bn_aggr(*a, **k))
do_bn_stats = later(lambda e, *a, **k: e.bn_stats(*a, **k))
do_dma_start = later(lambda e, *a, **k: e.dma_start(*a, **k))
do_indirect_dma_start = later(lambda e, *a, **k: e.indirect_dma_start(*a, **k))
do_matmul = later(lambda e, *a, **k: e.matmul(*a, **k))
do_memset = later(lambda e, *a, **k: e.memset(*a, **k))
do_partition_all_reduce = later(lambda e, *a, **k: e.partition_all_reduce(*a, **k))
do_reciprocal = later(lambda e, *a, **k: e.reciprocal(*a, **k))
do_scalar_tensor_tensor = later(lambda e, *a, **k: e.scalar_tensor_tensor(*a, **k))
do_tensor_copy = later(lambda e, *a, **k: e.tensor_copy(*a, **k))
do_tensor_reduce = later(lambda e, *a, **k: e.tensor_reduce(*a, **k))
do_tensor_scalar = later(lambda e, *a, **k: e.tensor_scalar(*a, **k))
do_tensor_tensor = later(lambda e, *a, **k: e.tensor_tensor(*a, **k))
do_tensor_tensor_reduce = later(lambda e, *a, **k: e.tensor_tensor_reduce(*a, **k))
do_transpose = later(lambda e, *a, **k: e.transpose(*a, **k))


class Engine:

    def __init__(self, sem):
        self.sem, self.n, self.ops = sem, 0, []

    def __call__(self, fn, *waits):
        self.n += 1
        self.ops.append((fn, [w for w in waits if w], self.sem, 1))
        return (self.sem, self.n)

    def quiet(self, fn, *waits):
        self.ops.append((fn, [w for w in waits if w], None, 0))

    def dma(self, fn, slot, *waits):
        slot[1] += 16
        self.ops.append((fn, [w for w in waits if w], slot[0], 16))
        return (slot[0], slot[1])

    def last(self):
        return (self.sem, self.n)

    def wait(self, *waits):
        self.ops.append((None, [w for w in waits if w], None, 0))

    def emit(self, e):
        seen = {}
        for fn, waits, sem, by in self.ops:
            for s, v in waits:
                if seen.get(id(s), 0) < v:
                    e.wait_ge(s, v)
                    seen[id(s)] = v
            if fn is not None:
                i = fn(e)
                if sem is not None:
                    i.then_inc(sem, by)


def decoder(nc, x_in, ctx_in, wqkv_in, wo_in, wg_in, wf_in, ident_in, mask_in, cos_in, sin_in, rank_in, tri_in, out):
    F32, F32R, BF16 = mybir.dt.float32, mybir.dt.float32r, mybir.dt.bfloat16
    I32 = mybir.dt.int32
    ALU, ACT, AX = mybir.AluOpType, mybir.ActivationFunctionType, mybir.AxisListType
    root = ExitStack()
    with root:
        def sem(name):
            return root.enter_context(nc.semaphore(name))

        pe, act, dve, pool, sp = (Engine(sem(f"s_{n}")) for n in ("pe", "act", "dve", "pool", "sp"))
        scope = [root]

        def sb(name, shape, dt=F32):
            return scope[-1].enter_context(nc.sbuf_tensor(name, shape, dt))

        def slot(name):
            return [sem(name), 0]

        bank = [root.enter_context(nc.psum_tensor(f"bank{i}", [128, 512], F32)) for i in range(8)]

        X = sb("X", [128, NT, D])
        XT = {b: sb(f"XT{b}", [128, 2, 4, 512], F32R) for b in (0, 2, 3)}
        ident = sb("ident", [128, 128])
        st = sb("st", [128, NT, 6])
        mv = sb("mv", [128, NT, 2])
        rstd = sb("rstd", [128, NT])
        rtmp = sb("rtmp", [128, NT])
        wam = sb("wam", [128, 4, 4])
        wsc = sb("wsc", [128, 2, 16])
        aam = sb("aam", [128, 4, 4])
        asc = sb("asc", [128, 4, 2, 4])
        s_x = [slot(f"s_x{i}") for i in range(NB)]
        s_c, s_i = slot("s_c"), slot("s_i")
        s_w = slot("s_w")

        t_x = []
        t_c = sp.dma(do_dma_start(ident[:, :], ident_in), s_i)
        xv = x_in.rearrange("(b i p) d -> b p i d", p=128, i=TB)
        for b in range(NB):
            t_x.append(sp.dma(do_dma_start(X[:, b * TB:(b + 1) * TB, :], xv[b]), s_x[b]))

        def rstd_of(ts, *waits):
            v, r, q = mv[:, ts, 1], rstd[:, ts], rtmp[:, ts]
            a = dve(do_tensor_scalar(v, v, EPS, None, ALU.add), *waits)
            a = dve(do_tensor_scalar(r.bitcast(I32), v.bitcast(I32), -0.5, float(0x5F3759DF), ALU.mult, ALU.add), a)
            for _ in range(3):
                a = dve(do_scalar_tensor_tensor(q, r, -0.5, r, ALU.mult, ALU.mult), a)
                a = dve(do_tensor_tensor(q, q, v, ALU.mult), a)
                a = dve(do_scalar_tensor_tensor(r, q, 1.5, r, ALU.add, ALU.mult), a)
            return a

        def stats_of(t, *waits):
            a = dve(do_bn_stats(st[:, t, :], X[:, t, :]), *waits)
            return dve(do_bn_aggr(mv[:, t, :], st[:, t, :]), a)

        def normed(dst, t, *waits):
            return dve(do_tensor_scalar(dst, X[:, t, :], mv[:, t, 0:1], rstd[:, t:t + 1],
                                                 ALU.subtract, ALU.mult), *waits)

        def transposed(src, ps, *waits):
            for c in range(3):
                pe.quiet(do_transpose(ps[:, c * 128:(c + 1) * 128], src[:, c * 128:(c + 1) * 128],
                                                    ident[:, :]), t_c, *(waits if not c else ()))
            return pe(do_transpose(ps[:, 384:512], src[:, 384:512], ident[:, :]))

        def split(dh, dl, ps, t_ps, *waits):
            h = act(do_activation(dh, ps, ACT.Copy), t_ps, *waits)
            l = dve(do_tensor_tensor(dl, ps, dh.bitcast(F32), ALU.subtract), h, *waits)
            return h, l

        phase = ExitStack()
        scope.append(phase)
        XT[1] = sb("XT1", [128, 2, 4, 512], F32R)
        Wraw = sb("Wraw", [128, 4, 384])
        Wh = sb("Wh", [128, 4, 384], F32R)
        Wl = sb("Wl", [128, 4, 384], F32R)
        QT = sb("QT", [128, 2, HG, 512], F32R)
        KT = sb("KT", [128, 2, 2, 512], F32R)
        VS = sb("VS", [128, 3, TB, 2, DH], F32R)
        P = sb("P", [128, 3, 1280])
        PTh = sb("PTh", [128, 1536], F32R)
        PTl = sb("PTl", [128, 1536], F32R)
        Oraw = Wraw[:, :, :].rearrange("p c n -> p (c n)")[:, 0:2 * D].rearrange("p (c n) -> p c n", c=2)
        Oh = sb("Oh", [128, 2, D], F32R)
        Ol = sb("Ol", [128, 2, D], F32R)
        cosT = sb("cosT", [128, TB, DH])
        sinT = sb("sinT", [128, TB, DH])
        mask = sb("mask", [128, 512])
        ST = sb("ST", [128, 1, 6, 2, DH])
        r1 = sb("r1", [128, 1, 320])
        r2 = sb("r2", [128, 1, 320])
        mn = sb("mn", [128, 3, 4])
        rs = sb("rs", [128, 3, 4])
        ri = sb("ri", [128, 3, 4])
        Otmp = sb("Otmp", [64, 512])
        Opair = sb("Opair", [128, 512])
        OTh = sb("OTh", [128, 3, 512], F32R)
        OTl = sb("OTl", [128, 3, 512], F32R)
        xn = P[:, :, 0:512]

        t_tab = [sp.dma(do_dma_start(d, s), s_c)
                 for d, s in ((cosT[:, :, :], cos_in), (sinT[:, :, :], sin_in), (mask[:, :], mask_in))][-1]
        wq_t, wo_t = {}, {}
        t_wq, t_wo = {}, {}

        def load_wq(g, *waits):
            t_wq[g] = sp.dma(do_dma_start(Wraw[:, :, :], wqkv_in[g]), s_w, *waits)

        def load_wo(g, *waits):
            t_wo[g] = sp.dma(do_dma_start(Oraw, wo_in[g]), s_w, *waits)

        def split_w(raw, h, l, t_raw, last_use, halves=(0, 1)):
            done = []
            k = raw.shape[1] // 2
            for c in halves:
                s = slice(c * k, (c + 1) * k)
                a = act(do_activation(h[:, s, :], raw[:, s, :], ACT.Copy), t_raw, last_use)
                b = (pool, dve)[c](do_tensor_tensor(l[:, s, :], raw[:, s, :], h[:, s, :].bitcast(F32), ALU.subtract),
                                   a, last_use)
                done += [a, b]
            return tuple(done)

        load_wq(0)
        wq_t[0] = split_w(Wraw, Wh, Wl, t_wq[0], None)
        load_wo(0, *wq_t[0])
        wo_t[0] = split_w(Oraw, Oh, Ol, t_wo[0], None)
        load_wq(1, *wo_t[0])

        t_z = pool(do_memset(PTh[:, 1152:1280].bitcast(F32), 0.0))
        t_z = pool(do_memset(PTl[:, 1152:1280].bitcast(F32), 0.0))
        xt_t = {}
        xn_free = [None, None]
        bank_free = [()] * 8
        for b in range(NB):
            for i in range(TB):
                a = stats_of(b * TB + i, t_x[b])
            a = rstd_of(slice(b * TB, (b + 1) * TB), a)
            for i in range(TB):
                t = b * TB + i
                n = normed(xn[:, t % 2, :], t, a, xn_free[t % 2])
                k = 6 + t % 2
                p = transposed(xn[:, t % 2, :], bank[k], n, *bank_free[k])
                xn_free[t % 2] = p
                ps = bank[k][:, :].rearrange("p (c n) -> p c n", c=4)
                xt_t[t] = bank_free[k] = split(XT[b][:, 0, :, i * 128:(i + 1) * 128], XT[b][:, 1, :, i * 128:(i + 1) * 128], ps, p)

        units = [(g, b) for g in range(NG) for b in range(NB)]
        st_free = [(), ()]
        st_t = {}
        qt_t, kt_t, v_t = {}, {}, {}
        pv_done, s_done = {}, {}
        proj_last = [None]
        wo_last = [None]
        r_free = [None, None]

        pr_t = {}

        def next_wq(g, half):
            wq_t[g] = (wq_t[g] if half else ()) + split_w(Wraw, Wh, Wl, t_wq[g], proj_last[0], (half,))
            if half:
                load_wo(g, *wq_t[g])

        def next_wo(g, half):
            wo_t[g] = (wo_t[g] if half else ()) + split_w(Oraw, Oh, Ol, t_wo[g], wo_last[0], (half,))
            if half and g + 1 < NG:
                load_wq(g + 1, *wo_t[g])

        def project(u, i):
            g, b = units[u]
            t = b * TB + i
            k = 6
            ps = bank[k]
            w = [*wq_t[g][0:2], *xt_t[t], *bank_free[k]]
            for c in range(4):
                if c == 2:
                    w = wq_t[g][2:4]
                xh, xl = XT[b][:, 0, c, i * 128:(i + 1) * 128], XT[b][:, 1, c, i * 128:(i + 1) * 128]
                for n, (l, r) in enumerate(((xh, Wh), (xh, Wl), (xl, Wh))):
                    last = c == 3 and n == 2
                    (pe if last else pe.quiet)(
                        do_matmul(ps[:, 0:384], l, r[:, c, :], start=c == 0 and n == 0, stop=last), *w)
                    w = []
            proj_last[0] = pe.last()
            pr_t[u, i] = (k, pe.last())

        def value_hi(u, i):
            k, p = pr_t[u, i]
            pr_t[u, i] = (k, p, act(do_activation(VS[:, u % 3, i, 0, :], bank[k][:, 320:384], ACT.Copy), p,
                                    pv_done.get(4 * (u - 3) + 3)))

        def rotate(u, i):
            k, p, vh = pr_t[u, i]
            ps = bank[k]
            vs = VS[:, u % 3, i, :, :]
            vl = dve(do_tensor_tensor(vs[:, 1, :], ps[:, 320:384], vs[:, 0, :].bitcast(F32), ALU.subtract), vh,
                     pv_done.get(4 * (u - 3) + 3))
            s = 0
            a, bb = r1[:, s, :], r2[:, s, :]
            c1 = cosT[:, i, :].unsqueeze(1).to_broadcast([128, 5, DH])
            v5 = ps[:, 0:320].rearrange("p (h d) -> p h d", h=5)
            a5, b5 = a.rearrange("p (h d) -> p h d", h=5), bb.rearrange("p (h d) -> p h d", h=5)
            m = dve(do_tensor_tensor(a5, v5, c1, ALU.mult), p, t_tab, r_free[s])
            for o, f in ((0, 32), (32, 0)):
                sn = sinT[:, i, o:o + 32].unsqueeze(1).to_broadcast([128, 5, 32])
                m = dve(do_tensor_tensor(b5[:, :, o:o + 32], v5[:, :, f:f + 32], sn, ALU.mult))
            v_t[u, i] = (vh, vl)
            bank_free[k] = (m, vh, vl)
            st_t[u, i] = pool(do_tensor_tensor(a, a, bb, ALU.add), m)

        def parts_qk(u, i):
            s = 0
            a5 = r1[:, s, :].rearrange("p (h d) -> p h d", h=5)
            S = ST[:, s, :, :, :]
            hh = act(do_activation(S[:, 0:5, 0, :].bitcast(F32R), a5, ACT.Copy), st_t[u, i], *st_free[s])
            h2 = act(do_activation(S[:, 4, 1, :].bitcast(F32R), a5[:, 4, :], ACT.Copy))
            return hh, h2

        def parts_qk2(u, i, hh, h2):
            s = 0
            a5 = r1[:, s, :].rearrange("p (h d) -> p h d", h=5)
            S = ST[:, s, :, :, :]
            q2 = dve(do_tensor_tensor(S[:, 0:4, 1, :].bitcast(F32R), a5[:, 0:4, :], S[:, 0:4, 0, :], ALU.subtract), hh, *st_free[s])
            k2 = dve(do_tensor_tensor(S[:, 5, :, :].bitcast(F32R), a5[:, 4, :].unsqueeze(1).to_broadcast([128, 2, DH]),
                                      S[:, 4, 0, :].unsqueeze(1).to_broadcast([128, 2, DH]), ALU.subtract))
            r_free[s] = k2
            st_t[u, i] = (h2, k2)

        def turn(u, i, kv):
            s = 0
            ps = bank[7]
            w = [*st_t[u, i], *bank_free[7], t_c]
            js = (4, 5) if kv else (0, 1, 2, 3)
            for m, j in enumerate(js):
                src = ST[:, s, j, :, :].rearrange("p a d -> p (a d)")
                (pe.quiet if j != js[-1] else pe)(do_transpose(ps[:, m * 128:(m + 1) * 128], src, ident[:, :]), *w)
                w = []
            p = pe.last()
            free = s_done.get(4 * (u - 2) + 3)
            dst, t = (KT, kt_t) if kv else (QT, qt_t)
            t[u, i] = act(do_activation(dst[:, u % 2, :, i * 128:(i + 1) * 128],
                                        ps[:, 0:128 * len(js)].rearrange("p (h n) -> p h n", n=128), ACT.Copy), p, free)
            bank_free[7] = (t[u, i],)
            if kv:
                st_free[s] = (p,)

        off = [0, 128, 384, 768]

        def pt_part(T, part):
            if part == 0:
                return T[:, 0:512].rearrange("p (m n) -> p m n", n=128)
            v = T[:, 512:1536].rearrange("p (m a n) -> p m a n", a=2, n=128)
            return v[:, :, 0, :] if part == 1 else v[:, 0:2, 1, :]

        def pt_of(T, kb):
            return (T[:, 0:512], pt_part(T, 1)[:, 0:3, :], pt_part(T, 2), T[:, 1152:1408])[kb]
        sfree = [(), ()]
        sn = [0]
        p_t, e_t = {}, {}
        tr_done = {}
        ptbank_free = {2: (), 3: (), 4: ()}
        pt_t = {}
        o_free = [()]
        opair_free = [None]
        otmp_free = [None]
        ot_t, o_t, oj_t = {}, {}, {}

        def scores(h, qb):
            u, j = divmod(h, 4)
            kk = sn[0] % 2
            sn[0] += 1
            ps = bank[kk]
            n = max(256, (qb + 1) * 128)
            lhs = QT[:, u % 2, j, qb * 128:(qb + 1) * 128]
            need = [qt_t[u, qb]] + [kt_t[u, i] for i in range(n // 128)]
            pe.quiet(do_matmul(ps[:, 0:n], lhs, KT[:, u % 2, 0, 0:n], start=True, stop=False), *need, *sfree[kk])
            p = s_done[h] = pe(do_matmul(ps[:, 0:n], lhs, KT[:, u % 2, 1, 0:n], start=False, stop=True))
            n = (qb + 1) * 128
            z = h % 3
            pq = P[:, z, off[qb]:off[qb] + n]
            a = dve(do_tensor_tensor_reduce(pq, ps[:, 0:n], mask[:, 512 - n:512], -0.125, BIG, ALU.add, ALU.min,
                                            mn[:, z, qb:qb + 1]), p, t_tab, tr_done.get(h - 3))
            sfree[kk] = (a,)

            def exp():
                e_t[h, qb] = act(do_activation(pq, pq, ACT.Exp, bias=mn[:, z, qb:qb + 1], scale=-1.0,
                                               accum_out=rs[:, z, qb:qb + 1]), a)
            return exp

        def norm_p(h):
            z = h % 3
            r = dve(do_reciprocal(ri[:, z, :], rs[:, z, :]), *(e_t[h, qb] for qb in range(4)))
            for qb in range(4):
                n = (qb + 1) * 128
                pq = P[:, z, off[qb]:off[qb] + n]
                p_t[h, qb] = pool(do_tensor_tensor(pq, pq, ri[:, z, qb:qb + 1].to_broadcast([128, n]), ALU.mult), r)

        def turn_p(h, part):
            z = h % 3
            k = 2 + part
            ps = bank[k]
            todo = [[(0, qb) for qb in range(4)], [(1, 1), (1, 2), (1, 3), (3, 3)], [(2, 2), (2, 3)]][part]
            w = [p_t[h, qb] for _, qb in todo] + [*ptbank_free[k], t_c]
            for m, (kb, qb) in enumerate(todo):
                src = P[:, z, off[qb] + kb * 128:off[qb] + (kb + 1) * 128]
                (pe if m == len(todo) - 1 else pe.quiet)(
                    do_transpose(ps[:, m * 128:(m + 1) * 128], src, ident[:, :]), *w)
                w = []
            p = pe.last()
            tr_done[h] = p
            free = pv_done.get(h - 1)
            v = ps[:, 0:128 * len(todo)].rearrange("p (m n) -> p m n", n=128)
            hi = act(do_activation(pt_part(PTh, part), v, ACT.Copy), p, free)

            def rest():
                lo = dve(do_tensor_tensor(pt_part(PTl, part), v, pt_part(PTh, part).bitcast(F32), ALU.subtract), hi, free)
                ptbank_free[k] = pt_t[h, part] = (hi, lo)
            return rest

        def weigh(h):
            u, j = divmod(h, 4)
            ps = bank[5]
            need = [x for pt in range(3) for x in pt_t[h, pt]] + [x for i in range(4) for x in v_t[u, i]] + [t_z]
            w = [*need, *o_free[0]]
            seq = [(kb, T) for kb in range(4) for T in (PTh, PTl)]
            for m, (kb, T) in enumerate(seq):
                q0 = min(kb * 128, 256)
                lhs = VS[:, u % 3, kb, :, :].rearrange("p a d -> p (a d)")
                last = m == 7
                (pe if last else pe.quiet)(
                    do_matmul(ps[:, q0:512], lhs, pt_of(T, kb), start=m == 0, stop=last), *w)
                w = []
            p = pv_done[h] = pe.last()
            o_t[h] = act(do_activation(Otmp[:, :], ps[64:128, :], ACT.Copy), p, otmp_free[0])

        def join(h):
            u, j = divmod(h, 4)
            ps, a = bank[5], o_t[h]
            half = slice(64 * (j % 2), 64 * (j % 2) + 64)
            b = dve(do_tensor_tensor(Opair[half, :], ps[0:64, :], Otmp[:, :], ALU.add), a, opair_free[0])
            otmp_free[0] = b
            o_free[0] = (a, b)
            oj_t[h] = b

        wo_done = {}

        def ot_at(u, c):
            return 2 if c else u % 2

        def pair(h):
            u, j = divmod(h, 4)
            if j % 2:
                c, b = ot_at(u, j // 2), oj_t[h]
                free = wo_done.get((u - (1 if j == 3 else 2), 3))
                hh = act(do_activation(OTh[:, c, :], Opair[:, :], ACT.Copy), b, free)
                l = pool(do_tensor_tensor(OTl[:, c, :], Opair[:, :], OTh[:, c, :].bitcast(F32), ALU.subtract), hh, free)
                opair_free[0] = l
                ot_t[u, j // 2] = (hh, l)

        x_t = {}

        def attn_out(u, i):
            g, b = units[u]
            t = b * TB + i
            ps = bank[5]
            w = [*wo_t[g][0:2], *ot_t[u, 0], *ot_t[u, 1], *o_free[0]]
            for c in range(2):
                if c:
                    w = wo_t[g][2:4]
                oh, ol = (T[:, ot_at(u, c), i * 128:(i + 1) * 128] for T in (OTh, OTl))
                for n, (l, r) in enumerate(((oh, Oh), (oh, Ol), (ol, Oh))):
                    last = c == 1 and n == 2
                    (pe if last else pe.quiet)(
                        do_matmul(ps[:, :], l, r[:, c, :], start=c == 0 and n == 0, stop=last), *w)
                    w = []
            p = wo_last[0] = wo_done[u, i] = pe.last()
            x_t[t] = dve(do_tensor_tensor(X[:, t, :], X[:, t, :], ps[:, :], ALU.add), p, x_t.get(t))
            o_free[0] = (x_t[t],)

        tiles = [(u, i) for u in range(len(units)) for i in range(TB)]
        nh = 4 * len(units)

        def tile_at(n):
            return tiles[n] if 0 <= n < len(tiles) else None

        def step(h):
            new, rot, trn = tile_at(h + 6), tile_at(h + 5), tile_at(h + 4)
            wo_u, wo_m = divmod(h - 7, 4)
            wo_now = 0 <= wo_u < len(units)
            first_q = new and new[0] and new[1] == 0 and units[new[0]][1] == 0
            first_o = wo_now and wo_u and wo_m == 0 and units[wo_u][1] == 0

            def next_w(half):
                if first_q:
                    next_wq(units[new[0]][0], half)
                if first_o:
                    next_wo(units[wo_u][0], half)

            next_w(0)
            if 1 <= h <= nh:
                norm_p(h - 1)
            if rot:
                value_hi(*rot)
            if 0 <= h < nh:
                scores(h, 3)()
                exp2 = scores(h, 2)
            if trn:
                turn(*trn, False)
            if 0 <= h < nh:
                exp2()
            if 3 <= h < nh + 3:
                weigh(h - 3)
            next_w(1)
            if rot:
                rotate(*rot)
            back = 2 <= h < nh + 2
            if back:
                lo0 = turn_p(h - 2, 0)
            if 0 <= h < nh:
                scores(h, 1)()
            if 3 <= h < nh + 3:
                join(h - 3)
            if back:
                lo0()
                lo1 = turn_p(h - 2, 1)
            if trn:
                turn(*trn, True)
            if 0 <= h < nh:
                scores(h, 0)()
            if back:
                lo2 = turn_p(h - 2, 2)
                lo1()
            if rot:
                hh = parts_qk(*rot)
            if back:
                lo2()
            if rot:
                parts_qk2(*rot, *hh)
            if new:
                project(*new)
            if wo_now:
                attn_out(wo_u, wo_m)
            if 3 <= h < nh + 3:
                pair(h - 3)



        phase.close()
        phase = root.enter_context(ExitStack())
        scope[-1] = phase
        NP = 17
        UP = 11
        U32 = mybir.dt.uint32
        NR = 6
        work = sb("work", [128, 8, 512])
        RW = sb("RW", [128, NR, 512])
        hm = sb("hm", [128, 2, 256])
        Gh = sb("Gh", [128, 4, 128], F32R)
        Gl = sb("Gl", [128, 4, 128], F32R)
        XN = sb("XN", [128, TB, D])
        Uh = sb("Uh", [128, UP, 4, 128], F32R)
        Ul = sb("Ul", [128, UP, 4, 128], F32R)
        Dh = sb("Dh", [128, 6, 512], F32R)
        Dl = sb("Dl", [128, 6, 512], F32R)
        CTh, CTl = XT[0][:, 0, :, :], XT[0][:, 1, :, :]
        YTh, YTl = ([XT[2 + z][:, n, :, :] for z in range(2)] for n in range(2))
        CW = [work[:, k, :] for k in range(3)]
        T1 = [work[:, 3 + k, :] for k in range(3)]
        T2 = [work[:, 6 + k, :] for k in range(2)]
        Hh = sb("Hh", [128, 6, 256], F32R)
        Hl = sb("Hl", [128, 5, 256], F32R)
        LG = sb("LG", [128, 512])
        Graw = sb("Graw", [128, 4, 8])
        rank = sb("rank", [128, 8])
        tri = sb("tri", [128, 128])
        trib = sb("trib", [128, 128], BF16)
        oneb = sb("oneb", [128, 128], BF16)
        lg = sb("lg", [128, 32])
        le = sb("le", [128, NT * 8])
        lq = sb("lq", [128, 32])
        lp = sb("lp", [128, 32])
        ohb = sb("ohb", [128, 32], BF16)
        cum = sb("cum", [128, 5, 8], BF16)
        sm = sb("sm", [128, 4, 4])
        kp = sb("kp", [128, NT])
        gk = sb("gk", [128, NT])
        gs = sb("gs", [128, NT])
        sidx = sb("sidx", [128, NT], U32)
        gidx = sb("gidx", [128, NT], U32)
        xd = nc.dram_tensor("xd", (NE * CAP, D), F32).ap()
        oe = nc.dram_tensor("oe", (NE * CAP, D), F32).ap()

        s_r = [slot(f"s_r{i}") for i in range(NR)]
        s_k, s_cw = slot("s_k"), [slot(f"s_cw{i}") for i in range(3)]
        s_z, s_sc = slot("s_z"), slot("s_sc")
        s_xe = [slot("s_xe0"), slot("s_xe1")]
        s_oe = [slot("s_oe0"), slot("s_oe1")]
        s_g = [slot(f"s_g{i}") for i in range(4)]
        s_o = slot("s_o")
        bf = [()] * 8
        late = {}

        def product(ps, pairs, waits, start=True, stop=True):
            w = list(waits)
            for m, (l, r) in enumerate(pairs):
                f = pe if m == len(pairs) - 1 else pe.quiet
                f(do_matmul(ps, l, r, start=start and m == 0, stop=stop and m == len(pairs) - 1), *w)
                w = []
            return pe.last()

        def three(lh, ll, rh, rl):
            return [(lh, rh), (lh, rl), (ll, rh)]

        piece_t = {}
        raw_t = {}
        piece_free = {}
        ring = [0]
        ring_free = [()] * NR
        order = [(m, p) for m in range(NE + 1) for p in range(NP)]

        def load_next():
            if ring[0] < len(order):
                m, p = order[ring[0]]
                k = ring[0] % NR
                raw_t[m, p] = (k, sp.dma(do_dma_start(RW[:, k, :], wf_in[m, p]), s_r[k], *(ring_free[k] or late["w"])))
                ring[0] += 1

        def split_piece(m, p):
            k, t = raw_t[m, p]
            if p < UP:
                h, l = Uh[:, p, :, :].rearrange("p c n -> p (c n)"), Ul[:, p, :, :].rearrange("p c n -> p (c n)")
            else:
                h, l = Dh[:, p - UP, :], Dl[:, p - UP, :]
            free = [piece_free[p]] if p in piece_free else late["x" if p < UP else "all"]
            a = act(do_activation(h, RW[:, k, :], ACT.Copy), t, *free)
            b = (pool if p % 2 else dve)(do_tensor_tensor(l, RW[:, k, :], h.bitcast(F32), ALU.subtract), a, *free)
            piece_t[m, p] = (a, b)
            ring_free[k] = (b,)
            load_next()

        c_t, z_n = {}, []

        def zero_rows():
            xdz = xd.rearrange("(t p) d -> t p d", p=128)
            if not z_n:
                c_t["z"] = pool(do_memset(T1[0], 0.0), late["work"])
            for t in range(len(z_n), len(z_n) + 2):
                z_n.append(t)
                c_t["zero"] = t1_free[0] = sp.dma(do_dma_start(xdz[t], T1[0]), s_z, c_t["z"])

        def constants():
            w = late["all"]
            t_k = [sp.dma(do_dma_start(d, v), s_k, *w)
                   for d, v in ((Graw[:, :, :], wg_in), (rank[:, :], rank_in), (tri[:, :], tri_in))][-1]
            z = pool(do_memset(Gh[:, :, :].bitcast(F32), 0.0), *w)
            z1 = pool(do_memset(Gl[:, :, :].bitcast(F32), 0.0))
            c_t["one"] = pool(do_memset(oneb[:, :], 1.0))
            run_t[0] = pool(do_memset(cum[:, 0, :], 0.0))
            h = act(do_activation(Gh[:, :, 0:8], Graw[:, :, :], ACT.Copy), t_k, z)
            l = pool(do_tensor_tensor(Gl[:, :, 0:8], Graw[:, :, :], Gh[:, :, 0:8].bitcast(F32), ALU.subtract), h, z1)
            c_t["g"] = (h, l)
            c_t["tri"] = act(do_activation(trib[:, :], tri[:, :], ACT.Copy), t_k)
            c_t["rank"] = t_k

        cv = ctx_in.rearrange("(b i p) d -> b i p d", p=128, i=TB)
        cw_n, cw_free, cw_at = [0], [None] * 3, {}

        def load_cw(b, i, n):
            k = cw_n[0] % 3
            cw_n[0] += 1
            cw_at[b, i, n] = (k, sp.dma(do_dma_start(CW[k], cv[b, i]), s_cw[k], cw_free[k] or late["work"]))

        t2_n, t2_free = [0], [None, None]

        def scales(amax, r, d, least, *waits):
            a = dve(do_tensor_scalar(d, amax, least, None, ALU.max), *waits)
            a = dve(do_reciprocal(r, d), a)
            a = dve(do_tensor_scalar(r, r, 448.0, None, ALU.mult), a)
            return dve(do_tensor_scalar(d, d, 1.0 / 448.0, None, ALU.mult), a)

        def blocks(y):
            return y.rearrange("p (c n) -> p c n", c=4)

        def rounded(y, r, d, *waits):
            k = t2_n[0] % 2
            t2_n[0] += 1
            q = T2[k]
            a = dve(do_tensor_tensor(blocks(y), blocks(y), r.unsqueeze(2).to_broadcast([128, 4, 128]), ALU.mult), *waits)
            a = dve(do_tensor_scalar(q.bitcast(U32), y.bitcast(U32), 0x7F800000, None, ALU.bitwise_and), a,
                    t2_free[k] or late["work"])
            a = dve(do_tensor_scalar(q, q, 2.0 ** -6, 1.5 * 2.0 ** 20, ALU.max, ALU.mult), a)
            a = pool(do_tensor_tensor(y, y, q, ALU.add), a)
            a = t2_free[k] = pool(do_tensor_tensor(y, y, q, ALU.subtract), a)
            return pool(do_tensor_tensor(blocks(y), blocks(y), d.unsqueeze(2).to_broadcast([128, 4, 128]), ALU.mult), a)

        tb, tbanks = [0], [(6,)]

        def turned(src, dh, dl, wait, *free):
            k = tbanks[0][tb[0] % len(tbanks[0])]
            tb[0] += 1
            p = transposed(src, bank[k], wait, *bf[k])
            ps = bank[k][:, :].rearrange("p (c n) -> p c n", c=4)
            h = act(do_activation(dh, ps, ACT.Copy), p, *free)

            def rest():
                l = dve(do_tensor_tensor(dl, ps, dh.bitcast(F32), ALU.subtract), h, *free)
                bf[k] = (h, l)
                return h, l
            return p, rest

        ct_t, ct_free = {}, [None]
        k_t = {}

        def context_max(b, i):
            k, t = cw_at[b, i, 0]
            k_t[b, i] = cw_free[k] = dve(do_tensor_reduce(
                wam[:, i, :], CW[k].rearrange("p (c n) -> p c n", c=4), AX.X, ALU.max, apply_absolute_value=True), t)

        def context_all(b):
            k_t[b] = pool(do_partition_all_reduce(wsc[:, 0, :], wam[:, :, :].rearrange("p i c -> p (i c)"), 128,
                                                  bass.bass_isa.ReduceOp.max), *(k_t[b, i] for i in range(TB)), ct_free[0])

        def context_scales(b):
            k_t[b] = scales(wsc[:, 0, :], wsc[:, 1, :], wsc[:, 0, :], 1e-6, k_t[b])

        def context_round(b, i):
            k, t = cw_at[b, i, 1]
            k_t[b, i] = rounded(CW[k], wsc[:, 1, 4 * i:4 * i + 4], wsc[:, 0, 4 * i:4 * i + 4], t, k_t[b])

        def context_turn(b, i):
            k, _ = cw_at[b, i, 1]
            sl = slice(i * 128, (i + 1) * 128)
            cw_free[k], rest = turned(CW[k], CTh[:, :, sl], CTl[:, :, sl], k_t[b, i], ct_free[0])

            def end():
                ct_t[b, i] = rest()
            return end

        t1_free = [None] * 3
        yt_free = [None, None]
        q_t, x2_t, y_t, n2_t, n3_t = {}, {}, {}, {}, {}

        def stats2(b, i):
            n2_t[b] = stats_of(b * TB + i, x_t[b * TB + i])

        def norm2(b):
            n2_t[b] = rstd_of(slice(b * TB, (b + 1) * TB), n2_t[b])

        def cross_round(b, i):
            t = b * TB + i
            y = T1[t % 3]
            a = normed(y, t, n2_t[b], t1_free[t % 3] or late["work"])
            a = dve(do_tensor_reduce(aam[:, i, :], blocks(y), AX.X, ALU.max, apply_absolute_value=True), a)
            a = scales(aam[:, i, :], asc[:, i, 0, :], asc[:, i, 1, :], 1e-4, a)
            q_t[t] = rounded(y, asc[:, i, 0, :], asc[:, i, 1, :], a)

        def cross_turn(b, i):
            t, z = b * TB + i, b % 2
            sl = slice(i * 128, (i + 1) * 128)
            t1_free[t % 3], rest = turned(T1[t % 3], YTh[z][:, :, sl], YTl[z][:, :, sl], q_t[t], yt_free[z])

            def end():
                q_t[t] = rest()
            return end

        def cross_product(b, i):
            t, z = b * TB + i, b % 2
            sl = slice(i * 128, (i + 1) * 128)
            pairs = [x for c in range(4) for x in three(YTh[z][:, c, sl], YTl[z][:, c, sl], CTh[:, c, :], CTl[:, c, :])]
            p = product(bank[6][:, :], pairs, [*q_t[t], *(x for q in range(TB) for x in ct_t[b, q]), *bf[6]])
            y_t[t] = ct_free[0] = p

            def end():
                x2_t[t] = dve(do_tensor_tensor(X[:, t, :], X[:, t, :], bank[6][:, :], ALU.add), p)
                bf[6] = (x2_t[t],)
                n3_t[b * TB + i] = stats_of(t, x2_t[t])
            return end

        xn_free = [None]
        run_t = [None]
        scat = [None]
        ready_y = {}
        lg_t, lg_free = {}, [None]
        small_free = [None]
        mx, em, ps_, fl = (sm[:, j, :] for j in range(4))
        l3, q3, p3 = (v[:, :].rearrange("p (i e) -> p i e", e=8) for v in (lg, lq, lp))

        def wide(v):
            return v.unsqueeze(2).to_broadcast([128, 4, 8])

        def rstd3(b):
            n3_t[b, 0] = rstd_of(slice(b * TB, (b + 1) * TB), *(n3_t[b * TB + i] for i in range(TB)))

        def norm3(b, i):
            t = b * TB + i
            n3_t[t] = normed(XN[:, i, :], t, n3_t[b, 0], *([scat[0]] if scat[0] else late["x"]))

        def route_turn(b, i):
            t, z = b * TB + i, b % 2
            sl = slice(i * 128, (i + 1) * 128)
            _, rest = turned(XN[:, i, :], YTh[z][:, :, sl], YTl[z][:, :, sl], n3_t[t], y_t[t])

            def end():
                ready_y.setdefault(b, []).extend(rest())
            return end

        def logits(b):
            z = b % 2
            pairs = [x for c in range(4) for x in three(Gh[:, c, :], Gl[:, c, :], YTh[z][:, c, :], YTl[z][:, c, :])]
            p = product(bank[6][:, :], pairs, [*c_t["g"], *ready_y[b], *bf[6]])
            a = act(do_activation(LG[:, :], bank[6][:, :], ACT.Copy), p, lg_free[0], *late["all"])
            bf[6] = (a,)
            lg_t[b] = a

        def choose(b):
            a = lg_t[b]
            k = tbanks[0][tb[0] % len(tbanks[0])]
            tb[0] += 1
            lg_free[0] = p = transposed(LG, bank[k], a, *bf[k])
            e3 = le[:, b * 32:b * 32 + 32].rearrange("p (i e) -> p i e", e=8)
            rk = rank[:, :].unsqueeze(1).to_broadcast([128, 4, 8])
            a = dve(do_tensor_copy(l3, bank[k][:, :].rearrange("p (i n) -> p i n", i=4)[:, :, 0:8]), p, small_free[0])
            bf[k] = (a,)
            m = dve(do_tensor_reduce(mx, l3, AX.X, ALU.max), a)
            d = dve(do_tensor_tensor(e3, l3, wide(mx), ALU.subtract), m)
            q = dve(do_tensor_tensor(q3, l3, wide(mx), ALU.is_equal), m)
            q = dve(do_tensor_tensor(q3, q3, rk, ALU.mult), q, c_t["rank"])
            q = dve(do_tensor_reduce(em, q3, AX.X, ALU.min), q)
            oh = dve(do_tensor_tensor(q3, rk, wide(em), ALU.is_equal), q)
            ob = dve(do_tensor_copy(ohb[:, :], lq[:, :]), oh)
            r = run_t[0]
            for i in range(TB):
                r = dve(do_tensor_tensor(cum[:, i + 1, :], cum[:, i, :], lq[:, i * 8:(i + 1) * 8], ALU.add), oh, r)
            lg_t[b] = (d, ob, r)

        def place(b):
            ts = slice(b * TB, (b + 1) * TB)
            d, ob, r = lg_t[b]
            p = product(bank[6][:, 0:32], [(trib[:, :], ohb[:, :]), (oneb[:, :], cum[:, 0:4, :].rearrange("p i e -> p (i e)"))],
                        [ob, r, c_t["tri"], c_t["one"], *bf[6]])
            run_t[0] = dve(do_tensor_copy(cum[:, 0, :], cum[:, 4, :]), p, r)
            v = dve(do_tensor_tensor(p3, bank[6][:, 0:32].rearrange("p (i e) -> p i e", e=8), q3, ALU.mult), p)
            bf[6] = (v,)
            v = dve(do_tensor_reduce(ps_, p3, AX.X, ALU.add), v)
            h = dve(do_tensor_scalar(kp[:, ts], ps_, float(CAP), None, ALU.is_lt), v)
            v = dve(do_scalar_tensor_tensor(fl, em, float(CAP), ps_, ALU.mult, ALU.add), v)
            v = dve(do_tensor_scalar(fl, fl, 1.0, float(8 * CAP + 4096), ALU.mult, ALU.add), v)
            v = dve(do_scalar_tensor_tensor(fl, kp[:, ts], -4096.0, fl, ALU.mult, ALU.add), v, h)
            v1 = dve(do_tensor_copy(sidx[:, ts], fl), v)
            v2 = dve(do_tensor_scalar(gidx[:, ts], fl, float(NE * CAP - 1), None, ALU.min), v)
            small_free[0] = v2
            for i in range(TB):
                t = b * TB + i
                scat[0] = pool.dma(do_indirect_dma_start(
                    xd, bass.IndirectOffsetOnAxis(ap=sidx[:, t:t + 1], axis=0), XN[:, i, :], None,
                    bounds_check=NE * CAP - 1, oob_is_err=False), s_sc, v1, c_t["zero"])

        def gates():
            e3 = le[:, :].rearrange("p (t e) -> p t e", e=8)
            a = act(do_activation(le[:, :], le[:, :], ACT.Exp), dve.last())
            a = dve(do_tensor_reduce(gs[:, :], e3, AX.X, ALU.add), a)
            a = dve(do_reciprocal(gk[:, :], gs[:, :]), a)
            return dve(do_tensor_tensor(gk[:, :], gk[:, :], kp[:, :], ALU.mult), a)

        h_free = [()]
        hn = [0]
        hm_free = [None, None]
        MAIN = -6
        up_n = [0]

        def expert(m, yh, yl, ready, done, split_next):
            def piece(p):
                if split_next and m < NE:
                    split_piece(m + 1, p)

            ht = [[] for _ in range(6)]

            def parts(c, s, d):
                if c < 5:
                    h = act(do_activation(Hh[:, c, :], hm[:, s, :], ACT.Copy), d, *h_free[0])
                    l = dve(do_tensor_tensor(Hl[:, c, :], hm[:, s, :], Hh[:, c, :].bitcast(F32), ALU.subtract), h, *h_free[0])
                else:
                    h = act(do_activation(Hh[0:64, 5, :], hm[0:64, s, :], ACT.Copy), d, *h_free[0])
                    l = dve(do_tensor_tensor(Hh[64:128, 5, :], hm[0:64, s, :], Hh[0:64, 5, :].bitcast(F32), ALU.subtract),
                            h, *h_free[0])
                hm_free[s] = l
                ht[c] = [h, l]

            prev = None
            for c in range(6):
                k = (4, 5, 7)[up_n[0] % 3]
                up_n[0] += 1
                ps = bank[k]
                for n, q in enumerate((2 * c, 2 * c + 1) if c < 5 else (10,)):
                    pairs = [x for kc in range(4) for x in three(Uh[:, q, kc, :], Ul[:, q, kc, :], yh(kc), yl(kc))]
                    p = product(ps[:, 256 * n:256 * n + 256], pairs, [*ready, *piece_t[m, q], *bf[k]])
                    piece_free[q] = p
                if prev:
                    parts(*prev)
                s = hn[0] % 2
                hn[0] += 1
                if c < 5:
                    a = act(do_activation(hm[:, s, :], ps[:, 0:256], ACT.Silu), p, hm_free[s])
                    d = dve(do_tensor_tensor(hm[:, s, :], hm[:, s, :], ps[:, 256:512], ALU.mult), a, p)
                else:
                    a = act(do_activation(hm[0:64, s, :], ps[0:64, 0:256], ACT.Silu), p, hm_free[s])
                    d = dve(do_tensor_tensor(hm[0:64, s, :], hm[0:64, s, :], ps[64:128, 0:256], ALU.mult), a, p)
                bf[k] = (a, d)
                prev = (c, s, d)
                if c:
                    piece(2 * c - 2)
                    piece(2 * c - 1)
                yield
            parts(*prev)
            piece(10)
            dt = [x for q in range(UP, NP) for x in piece_t[m, q]]
            for i in range(2):
                sl = slice(i * 128, (i + 1) * 128)
                for c in range(5):
                    product(bank[2 + i][:, :], three(Hh[:, c, sl], Hl[:, c, sl], Dh[:, c, :], Dl[:, c, :]),
                            [*ht[c], *(dt if not c else ()), *(bf[2 + i] if not c else ())], start=not c, stop=False)
            yield
            for i in range(2):
                sl = slice(i * 128, (i + 1) * 128)
                p = product(bank[2 + i][:, :], [(Hh[:, 5, sl], Dh[:, 5, :]), (Hh[:, 5, sl], Dl[:, 5, :])], ht[5], start=False)
                bf[2 + i] = (done(i, 2 + i, p),)
            h_free[0] = (p,)
            for q in range(UP, NP):
                piece_free[q] = p
            for q in range(UP, NP):
                piece(q)
            yield

        def shared(b, half, split_next):
            z = b % 2
            o = half * 256

            def done(i, k, p):
                t = b * TB + 2 * half + i
                x2_t[t] = dve(do_tensor_tensor(X[:, t, :], X[:, t, :], bank[k][:, :], ALU.add), p, x2_t[t])
                return x2_t[t]

            yield from expert(0, lambda kc: YTh[z][:, kc, o:o + 256], lambda kc: YTl[z][:, kc, o:o + 256], ready_y[b], done,
                              split_next)
            yt_free[z] = pe.last()

        xe_t, xt_e = {}, {}
        XE = XN[:, :, :].rearrange("p (z i) d -> p z i d", z=2)
        xdv = xd.rearrange("(m i p) d -> m p i d", p=128, i=2)
        oev = oe.rearrange("(m i p) d -> m i p d", p=128, i=2)
        xe_free = [None, None]

        def load_x(m):
            xe_t[m] = sp.dma(do_dma_start(XE[:, m % 2, :, :], xdv[m]), s_xe[m % 2], xe_free[m % 2], scat[0])

        def turn_x(m, i):
            z = m % 2
            sl = slice(i * 128, (i + 1) * 128)
            xe_free[z], rest = turned(XE[:, z, i, :], YTh[z][:, :, sl], YTl[z][:, :, sl], xe_t[m], yt_free[z])
            xt_e.setdefault(m, []).extend(rest())

        side = {}

        def plan(s, f, *a):
            side.setdefault(s, []).append((f, a))

        def plan_context(b, s):
            def first(i):
                context_max(b, i)
                load_cw(b, *((3, 0) if i == 0 else (i - 1, 1)))

            def turn_and_load(i):
                end = context_turn(b, i)
                if i == 0:
                    load_cw(b, 3, 1)
                elif b + 1 < NB:
                    load_cw(b + 1, i - 1, 0)
                return end

            for i in range(TB):
                plan(s + i // 2, first, i)
            plan(s + 2, context_all, b)
            plan(s + 3, context_scales, b)
            for i in range(TB):
                at = s + 4 + i + i // 3
                plan(at, context_round, b, i)
                plan(at + 2, turn_and_load, i)

        def plan_cross(b, s):
            for i in range(TB):
                plan(s - 13 + i if b else s - 3 + i // 2, stats2, b, i)
                plan(s + 1 + i, cross_turn, b, i)
                plan(s + 2 + i, cross_product, b, i)
                plan(s - 1 + i, cross_round, b, i)
                plan(s + 7 + i // 2, norm3, b, i)
                plan(s + 8 + i // 2, route_turn, b, i)
            plan(s - (7 if b else 2), norm2, b)
            plan(s + 6, rstd3, b)
            plan(s + 10, logits, b)
            plan(s + 13, choose, b)
            plan(s + 19, place, b)

        for b in range(NB):
            plan_cross(b, 16 * (b - 1))
            plan_context(b, 16 * (b - 1) - 10)

        kinds = [route_turn, cross_turn, logits, choose, place, cross_product]

        for i in range(2):
            plan(16 * NB - 10, load_x, i)
            plan(16 * NB - 8 + i, turn_x, 0, i)

        def run_slot(s):
            fs = side.pop(s, [])
            fs.sort(key=lambda fa: kinds.index(fa[0]) if fa[0] in kinds else len(kinds) - (fa[0].__name__ == "turn_and_load") * 9)
            for g in [g for g in [f(*a) for f, a in fs] if g]:
                g()

        pieces = list(range(NP))

        def split_first(n):
            for _ in range(min(n, len(pieces))):
                split_piece(0, pieces.pop(0))

        slot_n = -26
        for h in range(-6, nh + 7):
            step(h)
            if h == nh - 19:
                ct_free[0] = proj_last[0]
            if h == nh - 14:
                late["work"] = proj_last[0]
                for i in range(3):
                    load_cw(0, i, 0)
            if nh - 12 <= h < nh - 4:
                zero_rows()
            if h == nh - 11:
                yt_free[0] = proj_last[0]
            if h == nh - 6:
                yt_free[1] = proj_last[0]
                bf[6] = bank_free[6]
                late["w"] = (proj_last[0], *wo_t[NG - 1])
                for _ in range(NR):
                    load_next()
            if h == nh - 1:
                bf[0], bf[1] = sfree
                tbanks[0] = (0, 1)
            if h == nh + 2:
                late["x"] = [x.last() for x in (pe, act, dve, pool)]
            if h >= nh - 12:
                run_slot(slot_n)
                slot_n += 1
        late["all"] = [x.last() for x in (pe, act, dve, pool)]
        h_free[0] = tuple(late["all"])
        for k in (2, 3, 4, 5, 7):
            bf[k] = tuple(late["all"])
        constants()
        while slot_n < MAIN:
            split_first(4)
            run_slot(slot_n)
            slot_n += 1
        split_first(NP)
        for b in range(NB):
            for half in range(2):
                g = shared(b, half, b == NB - 1 and half == 1)
                for _ in range(8):
                    run_slot(slot_n)
                    slot_n += 1
                    next(g)
                for _ in g:
                    pass
        assert not side

        OE = T2
        oe_free = list(t2_free)
        t_gk = gates()
        for m in range(NE):
            z = m % 2

            def done(i, k, p):
                r = act(do_activation(OE[i], bank[k][:, :], ACT.Copy), p, oe_free[i])
                oe_free[i] = sp.dma(do_dma_start(oev[m, i], OE[i]), s_oe[i], r)
                return r

            for n, _ in enumerate(expert(m + 1, lambda kc: YTh[z][:, kc, 0:256], lambda kc: YTl[z][:, kc, 0:256],
                                         xt_e[m], done, True)):
                if n in (1, 2) and m + 1 < NE:
                    turn_x(m + 1, n - 1)
                if n == 2 and m + 2 < NE:
                    load_x(m + 2)
            yt_free[z] = pe.last()

        G = XN
        ov = out.rearrange("(t p) d -> t p d", p=128)
        g_free = [(xe_free[0], xe_free[1])] * 4
        for t in range(NT):
            k = t % 4
            g = pool.dma(do_indirect_dma_start(G[:, k, :], None, oe, bass.IndirectOffsetOnAxis(ap=gidx[:, t:t + 1], axis=0)),
                         s_g[k], *oe_free, *g_free[k])
            x = dve(do_scalar_tensor_tensor(X[:, t, :], G[:, k, :], gk[:, t:t + 1], X[:, t, :], ALU.mult, ALU.add),
                    g, x2_t[t], t_gk)
            g_free[k] = (x,)
            sp.dma(do_dma_start(ov[t], X[:, t, :]), s_o, x)
        sp.wait((s_o[0], s_o[1]))

        with nc.Block() as block:
            block.tensor(pe.emit)
            block.scalar(act.emit)
            block.vector(dve.emit)
            block.gpsimd(pool.emit)
            block.sync(sp.emit)


def kernel(**inputs):
    import concourse.bacc as bacc
    from concourse import mybir as mb
    from concourse.bass_utils import run_bass_kernel_spmd as run

    f = np.float32
    a = {k: np.asarray(v) for k, v in inputs.items()}
    pos = np.arange(512, dtype=f)
    freq = (10000.0 ** (-np.arange(0, 64, 2, dtype=np.float64) / 64)).astype(f)
    theta = np.outer(pos, freq).astype(f).astype(np.float64)
    c, s = np.cos(theta).astype(f), np.sin(theta).astype(f)
    tab = lambda m: np.ascontiguousarray(m.reshape(4, 128, 64).transpose(1, 0, 2))
    mask = np.zeros((128, 512), f)
    mask[:, 384:] = np.where(np.arange(128)[None, :] > np.arange(128)[:, None], f(-BIG), f(0))
    kc = lambda w: np.ascontiguousarray(w.reshape(w.shape[0] // 128, 128, w.shape[1]).transpose(1, 0, 2))
    wq, wk, wv, wo = (a[f"L0_attn_{n}"] for n in ("wq", "wk", "wv", "wo"))
    wqkv = np.stack([kc(np.concatenate([wq[:, 256 * g:256 * g + 256], wk[:, 64 * g:64 * g + 64],
                                        wv[:, 64 * g:64 * g + 64]], axis=1)) for g in range(NG)])
    wog = np.stack([kc(wo[256 * g:256 * g + 256]) for g in range(NG)])

    def cut(w1, w3, w2):
        cols = [w[:, 128 * n:128 * n + 128] for n in range(5) for w in (w1, w3)]
        cols.append(np.concatenate([w1[:, 640:], w3[:, 640:]], axis=1))
        rows = [w2[128 * n:128 * n + 128] for n in range(5)] + [np.concatenate([w2[640:], w2[640:]])]
        return np.stack([kc(w).reshape(128, 512) for w in cols] + rows)

    fw = [a[f"L0_ffn_{n}"] for n in ("W1", "W3", "W2")]
    pieces = np.stack([cut(*(a[f"L0_ffn_{n}"] for n in ("sw1", "sw3", "sw2")))] + [cut(*(w[m] for w in fw)) for m in range(NE)])
    arrays = {
        "x": np.ascontiguousarray(a["x"].reshape(2048, 512)),
        "ctx": np.ascontiguousarray(a["ctx_2048"].reshape(2048, 512)),
        "wqkv": wqkv, "wo": wog,
        "wg": kc(a["L0_ffn_Wg"]), "wf": pieces,
        "ident": np.eye(128, dtype=f), "mask": mask,
        "cos": tab(np.concatenate([c, c], 1)), "sin": tab(np.concatenate([-s, s], 1)),
        "rank": np.tile(np.arange(-8, 0, dtype=f), (128, 1)),
        "tri": np.triu(np.ones((128, 128), f), 1),
    }
    nc = bacc.Bacc("TRN2", target_bir_lowering=False, num_devices=1)
    args = [nc.dram_tensor(f"in_{k}", v.shape, mb.dt.float32, kind="ExternalInput").ap() for k, v in arrays.items()]
    o = nc.dram_tensor("out", (2048, 512), mb.dt.float32, kind="ExternalOutput").ap()
    decoder(nc, *args, o)
    r = run(nc, [{f"in_{k}": v for k, v in arrays.items()}], core_ids=[0])
    return r.results[0]["out"].reshape(4, 512, 512)
```

```python
import numpy as np
import concourse.bass as bass
from concourse import mybir
from contextlib import ExitStack

NT, D, NB, TB = 16, 512, 4, 4
NG, HG, DH = 8, 4, 64
NE, CAP, HID = 8, 256, 704
EPS = 1e-5
BIG = 1e30


def later(fn):
    def make(*args, **kw):
        return lambda e: fn(e, *args, **kw)
    return make


do_activation = later(lambda e, *a, **k: e.activation(*a, **k))
do_bn_aggr = later(lambda e, *a, **k: e.bn_aggr(*a, **k))
do_bn_stats = later(lambda e, *a, **k: e.bn_stats(*a, **k))
do_dma_start = later(lambda e, *a, **k: e.dma_start(*a, **k))
do_indirect_dma_start = later(lambda e, *a, **k: e.indirect_dma_start(*a, **k))
do_matmul = later(lambda e, *a, **k: e.matmul(*a, **k))
do_memset = later(lambda e, *a, **k: e.memset(*a, **k))
do_partition_all_reduce = later(lambda e, *a, **k: e.partition_all_reduce(*a, **k))
do_reciprocal = later(lambda e, *a, **k: e.reciprocal(*a, **k))
do_scalar_tensor_tensor = later(lambda e, *a, **k: e.scalar_tensor_tensor(*a, **k))
do_tensor_copy = later(lambda e, *a, **k: e.tensor_copy(*a, **k))
do_tensor_reduce = later(lambda e, *a, **k: e.tensor_reduce(*a, **k))
do_tensor_scalar = later(lambda e, *a, **k: e.tensor_scalar(*a, **k))
do_tensor_tensor = later(lambda e, *a, **k: e.tensor_tensor(*a, **k))
do_tensor_tensor_reduce = later(lambda e, *a, **k: e.tensor_tensor_reduce(*a, **k))
do_transpose = later(lambda e, *a, **k: e.transpose(*a, **k))


class Engine:

    def __init__(self, sem):
        self.sem, self.n, self.ops = sem, 0, []

    def __call__(self, fn, *waits):
        self.n += 1
        self.ops.append((fn, [w for w in waits if w], self.sem, 1))
        return (self.sem, self.n)

    def quiet(self, fn, *waits):
        self.ops.append((fn, [w for w in waits if w], None, 0))

    def dma(self, fn, slot, *waits):
        slot[1] += 16
        self.ops.append((fn, [w for w in waits if w], slot[0], 16))
        return (slot[0], slot[1])

    def last(self):
        return (self.sem, self.n)

    def wait(self, *waits):
        self.ops.append((None, [w for w in waits if w], None, 0))

    def emit(self, e):
        seen = {}
        for fn, waits, sem, by in self.ops:
            for s, v in waits:
                if seen.get(id(s), 0) < v:
                    e.wait_ge(s, v)
                    seen[id(s)] = v
            if fn is not None:
                i = fn(e)
                if sem is not None:
                    i.then_inc(sem, by)


def decoder(nc, x_in, ctx_in, wqkv_in, wo_in, wg_in, wf_in, ident_in, mask_in, cos_in, sin_in, rank_in, tri_in, out):
    F32, F32R, BF16 = mybir.dt.float32, mybir.dt.float32r, mybir.dt.bfloat16
    I32 = mybir.dt.int32
    ALU, ACT, AX = mybir.AluOpType, mybir.ActivationFunctionType, mybir.AxisListType
    root = ExitStack()
    with root:
        def sem(name):
            return root.enter_context(nc.semaphore(name))

        pe, act, dve, pool, sp = (Engine(sem(f"s_{n}")) for n in ("pe", "act", "dve", "pool", "sp"))
        scope = [root]

        def sb(name, shape, dt=F32):
            return scope[-1].enter_context(nc.sbuf_tensor(name, shape, dt))

        def slot(name):
            return [sem(name), 0]

        bank = [root.enter_context(nc.psum_tensor(f"bank{i}", [128, 512], F32)) for i in range(8)]

        X = sb("X", [128, NT, D])
        XT = {b: sb(f"XT{b}", [128, 2, 4, 512], F32R) for b in (0, 2, 3)}
        ident = sb("ident", [128, 128])
        st = sb("st", [128, NT, 6])
        mv = sb("mv", [128, NT, 2])
        rstd = sb("rstd", [128, NT])
        rtmp = sb("rtmp", [128, NT])
        wam = sb("wam", [128, 4, 4])
        wsc = sb("wsc", [128, 2, 16])
        aam = sb("aam", [128, 4, 4])
        asc = sb("asc", [128, 4, 2, 4])
        s_x = [slot(f"s_x{i}") for i in range(TB + NB)]
        s_c, s_i = slot("s_c"), slot("s_i")
        s_w = slot("s_w")

        t_x = {}
        xv = x_in.rearrange("(b i p) d -> b p i d", p=128, i=TB)
        for i in range(TB):
            t_x[i] = sp.dma(do_dma_start(X[:, i, :], xv[0, :, i, :]), s_x[i])
        t_c = sp.dma(do_dma_start(ident[:, :], ident_in), s_i)

        def rstd_of(ts, *waits):
            v, r, q = mv[:, ts, 1], rstd[:, ts], rtmp[:, ts]
            a = dve(do_tensor_scalar(v, v, EPS, None, ALU.add), *waits)
            a = dve(do_tensor_scalar(r.bitcast(I32), v.bitcast(I32), -0.5, float(0x5F3759DF), ALU.mult, ALU.add), a)
            for _ in range(3):
                a = dve(do_scalar_tensor_tensor(q, r, -0.5, r, ALU.mult, ALU.mult), a)
                a = dve(do_tensor_tensor(q, q, v, ALU.mult), a)
                a = dve(do_scalar_tensor_tensor(r, q, 1.5, r, ALU.add, ALU.mult), a)
            return a

        def stats_of(t, *waits):
            a = dve(do_bn_stats(st[:, t, :], X[:, t, :]), *waits)
            return dve(do_bn_aggr(mv[:, t, :], st[:, t, :]), a)

        def normed(dst, t, *waits):
            return dve(do_tensor_scalar(dst, X[:, t, :], mv[:, t, 0:1], rstd[:, t:t + 1],
                                                 ALU.subtract, ALU.mult), *waits)

        def transposed(src, ps, *waits):
            for c in range(3):
                pe.quiet(do_transpose(ps[:, c * 128:(c + 1) * 128], src[:, c * 128:(c + 1) * 128],
                                                    ident[:, :]), t_c, *(waits if not c else ()))
            return pe(do_transpose(ps[:, 384:512], src[:, 384:512], ident[:, :]))

        def split(dh, dl, ps, t_ps, *waits):
            h = act(do_activation(dh, ps, ACT.Copy), t_ps, *waits)
            l = dve(do_tensor_tensor(dl, ps, dh.bitcast(F32), ALU.subtract), h, *waits)
            return h, l

        phase = ExitStack()
        scope.append(phase)
        XT[1] = sb("XT1", [128, 2, 4, 512], F32R)
        Wraw = sb("Wraw", [128, 4, 384])
        Wh = sb("Wh", [128, 4, 384], F32R)
        Wl = sb("Wl", [128, 4, 384], F32R)
        QT = sb("QT", [128, 2, HG, 512], F32R)
        KT = sb("KT", [128, 2, 2, 512], F32R)
        VS = sb("VS", [128, 3, TB, 2, DH], F32R)
        P = sb("P", [128, 3, 1280])
        PTh = sb("PTh", [128, 1536], F32R)
        PTl = sb("PTl", [128, 1536], F32R)
        Oraw = Wraw[:, :, :].rearrange("p c n -> p (c n)")[:, 0:2 * D].rearrange("p (c n) -> p c n", c=2)
        Oh = sb("Oh", [128, 2, D], F32R)
        Ol = sb("Ol", [128, 2, D], F32R)
        cosT = sb("cosT", [128, TB, DH])
        sinT = sb("sinT", [128, TB, DH])
        mask = sb("mask", [128, 512])
        ST = sb("ST", [128, 6, 2, DH])
        r1 = sb("r1", [128, 320])
        r2 = sb("r2", [128, 320])
        mn = sb("mn", [128, 3, 4])
        rs = sb("rs", [128, 3, 4])
        ri = sb("ri", [128, 3, 4])
        Otmp = sb("Otmp", [64, 512])
        Opair = sb("Opair", [128, 512])
        OTh = sb("OTh", [128, 3, 512], F32R)
        OTl = sb("OTl", [128, 3, 512], F32R)

        wq_t, wo_t = {}, {}
        t_wq, t_wo = {}, {}

        def load_wq(g, *waits):
            t_wq[g] = sp.dma(do_dma_start(Wraw[:, :, :], wqkv_in[g]), s_w, *waits)

        def load_wo(g, *waits):
            t_wo[g] = sp.dma(do_dma_start(Oraw, wo_in[g]), s_w, *waits)

        def split_hi(raw, h, half, *waits):
            k = raw.shape[1] // 2
            sl = slice(half * k, half * k + k)
            return act(do_activation(h[:, sl, :], raw[:, sl, :], ACT.Copy), *waits)

        def split_lo(engine, raw, h, l, half, *waits):
            k = raw.shape[1] // 2
            sl = slice(half * k, half * k + k)
            return engine(do_tensor_tensor(l[:, sl, :], raw[:, sl, :], h[:, sl, :].bitcast(F32), ALU.subtract), *waits)

        def split_w(raw, h, l, t_raw, engines):
            done = ()
            for half in range(2):
                a = split_hi(raw, h, half, t_raw)
                done += (a, split_lo(engines[half], raw, h, l, half, a))
            return done

        def split_stage(stage, done, raw, h, l, t_raw, last_use):
            if stage < 2:
                done += (split_hi(raw, h, stage, t_raw, last_use),)
            if stage != 1:
                done += (split_lo(dve if stage else pool, raw, h, l, stage // 2, done[-1], last_use),)
            return done

        def load_x_of(b):
            t = sp.dma(do_dma_start(X[:, b * TB:(b + 1) * TB, :], xv[b]), s_x[TB + b])
            for i in range(TB):
                t_x[b * TB + i] = t

        load_wq(0)
        load_x_of(1)
        t_tab = [sp.dma(do_dma_start(d, s), s_c)
                 for d, s in ((cosT[:, :, :], cos_in), (sinT[:, :, :], sin_in), (mask[:, :], mask_in))][-1]
        load_x_of(2)
        load_x_of(3)
        t_z = pool(do_memset(PTh[:, 1152:1280].bitcast(F32), 0.0))
        t_z = pool(do_memset(PTl[:, 1152:1280].bitcast(F32), 0.0))
        xt_t, n1_t = {}, {}
        xn = [P[:, z, 512 * e:512 * e + 512] for z in range(3) for e in range(2)]
        xn.append(Wraw[:, :, :].rearrange("p c n -> p (c n)")[:, 2 * D:])
        xn_free = [None] * 7
        bank_free = [()] * 8

        def first_stats(t):
            n1_t[t] = stats_of(t, t_x[t])

        def first_rstd(b, e):
            a = rstd_of(slice(b * TB, e * TB), n1_t[e * TB - 1])
            for t in range(b * TB, e * TB):
                n1_t[t] = a

        def first_norm(t):
            m = t if t < 4 else 4 + t % 2 if t < 8 else 6
            n1_t[t] = (m, normed(xn[m], t, n1_t[t], xn_free[m], *(wq_t[0] if m == 6 else ())))

        def first_turn(t, k, free):
            m, n = n1_t[t]
            b, i = divmod(t, TB)
            p = xn_free[m] = transposed(xn[m], bank[k], n, *free)
            ps = bank[k][:, :].rearrange("p (c n) -> p c n", c=4)
            sl = slice(i * 128, (i + 1) * 128)
            xt_t[t] = split(XT[b][:, 0, :, sl], XT[b][:, 1, :, sl], ps, p)
            return xt_t[t]

        for t in range(TB):
            first_stats(t)
        first_rstd(0, 1)
        for t in range(TB):
            first_norm(t)
        wq_t[0] = split_w(Wraw, Wh, Wl, t_wq[0], (pool, pool))
        load_wo(0, *wq_t[0])
        for t in range(TB):
            bank_free[t] = first_turn(t, t, ())
        for t in range(TB, 2 * TB):
            first_stats(t)

        units = [(g, b) for g in range(NG) for b in range(NB)]
        st_free = [()]
        st_t = {}
        qt_t, kt_t, v_t = {}, {}, {}
        pv_done, s_done = {}, {}
        proj_last = [None]
        wo_last = [None]
        r_free = [None]

        pr_t = {}

        def next_wq(g, stage):
            wq_t[g] = split_stage(stage, wq_t.get(g, ()), Wraw, Wh, Wl, t_wq[g], proj_last[0])
            if stage == 2:
                load_wo(g, *wq_t[g])

        def next_wo(g, stage):
            wo_t[g] = split_stage(stage, wo_t.get(g, ()), Oraw, Oh, Ol, t_wo[g], wo_last[0])
            if stage == 2 and g + 1 < NG:
                load_wq(g + 1, *wo_t[g])

        def project(u, i):
            g, b = units[u]
            t = b * TB + i
            k = 4 if u * TB + i in (1, 3, 5) else 6
            ps = bank[k]
            w = [*wq_t[g][0:2], *xt_t[t], *bank_free[k]]
            for c in range(4):
                if c == 2:
                    w = wq_t[g][2:4]
                xh, xl = XT[b][:, 0, c, i * 128:(i + 1) * 128], XT[b][:, 1, c, i * 128:(i + 1) * 128]
                for n, (l, r) in enumerate(((xh, Wh), (xh, Wl), (xl, Wh))):
                    last = c == 3 and n == 2
                    (pe if last else pe.quiet)(
                        do_matmul(ps[:, 0:384], l, r[:, c, :], start=c == 0 and n == 0, stop=last), *w)
                    w = []
            proj_last[0] = pe.last()
            pr_t[u, i] = (k, pe.last())

        def value_hi(u, i):
            k, p = pr_t[u, i]
            pr_t[u, i] = (k, p, act(do_activation(VS[:, u % 3, i, 0, :], bank[k][:, 320:384], ACT.Copy), p,
                                    pv_done.get(4 * (u - 3) + 3)))

        def rotate(u, i):
            k, p, vh = pr_t[u, i]
            ps = bank[k]
            vs = VS[:, u % 3, i, :, :]
            vl = dve(do_tensor_tensor(vs[:, 1, :], ps[:, 320:384], vs[:, 0, :].bitcast(F32), ALU.subtract), vh,
                     pv_done.get(4 * (u - 3) + 3))
            a, bb = r1[:, :], r2[:, :]
            c1 = cosT[:, i, :].unsqueeze(1).to_broadcast([128, 5, DH])
            v5 = ps[:, 0:320].rearrange("p (h d) -> p h d", h=5)
            a5, b5 = a.rearrange("p (h d) -> p h d", h=5), bb.rearrange("p (h d) -> p h d", h=5)
            m = dve(do_tensor_tensor(a5, v5, c1, ALU.mult), p, t_tab, r_free[0])
            for o, f in ((0, 32), (32, 0)):
                sn = sinT[:, i, o:o + 32].unsqueeze(1).to_broadcast([128, 5, 32])
                m = dve(do_tensor_tensor(b5[:, :, o:o + 32], v5[:, :, f:f + 32], sn, ALU.mult))
            v_t[u, i] = (vh, vl)
            bank_free[k] = (m, vh, vl)
            st_t[u, i] = pool(do_tensor_tensor(a, a, bb, ALU.add), m)

        def parts_qk(u, i):
            a5 = r1[:, :].rearrange("p (h d) -> p h d", h=5)
            S = ST[:, :, :, :]
            hh = act(do_activation(S[:, 0:5, 0, :].bitcast(F32R), a5, ACT.Copy), st_t[u, i], *st_free[0])
            h2 = act(do_activation(S[:, 4, 1, :].bitcast(F32R), a5[:, 4, :], ACT.Copy))
            return hh, h2

        def parts_qk2(u, i, hh, h2):
            a5 = r1[:, :].rearrange("p (h d) -> p h d", h=5)
            S = ST[:, :, :, :]
            q2 = dve(do_tensor_tensor(S[:, 0:4, 1, :].bitcast(F32R), a5[:, 0:4, :], S[:, 0:4, 0, :], ALU.subtract), hh, *st_free[0])
            k2 = dve(do_tensor_tensor(S[:, 5, :, :].bitcast(F32R), a5[:, 4, :].unsqueeze(1).to_broadcast([128, 2, DH]),
                                      S[:, 4, 0, :].unsqueeze(1).to_broadcast([128, 2, DH]), ALU.subtract))
            r_free[0] = k2
            st_t[u, i] = (h2, k2)

        def turn(u, i, kv):
            ps = bank[7]
            w = [*st_t[u, i], *bank_free[7], t_c]
            js = (4, 5) if kv else (0, 1, 2, 3)
            for m, j in enumerate(js):
                src = ST[:, j, :, :].rearrange("p a d -> p (a d)")
                (pe.quiet if j != js[-1] else pe)(do_transpose(ps[:, m * 128:(m + 1) * 128], src, ident[:, :]), *w)
                w = []
            p = pe.last()
            free = s_done.get(4 * (u - 2) + 3)
            dst, t = (KT, kt_t) if kv else (QT, qt_t)
            t[u, i] = act(do_activation(dst[:, u % 2, :, i * 128:(i + 1) * 128],
                                        ps[:, 0:128 * len(js)].rearrange("p (h n) -> p h n", n=128), ACT.Copy), p, free)
            bank_free[7] = (t[u, i],)
            if kv:
                st_free[0] = (p,)

        off = [0, 128, 384, 768]

        def pt_part(T, part):
            if part == 0:
                return T[:, 0:512].rearrange("p (m n) -> p m n", n=128)
            v = T[:, 512:1536].rearrange("p (m a n) -> p m a n", a=2, n=128)
            return v[:, :, 0, :] if part == 1 else v[:, 0:2, 1, :]

        def pt_of(T, kb):
            return (T[:, 0:512], pt_part(T, 1)[:, 0:3, :], pt_part(T, 2), T[:, 1152:1408])[kb]
        sfree = [(), ()]
        sn = [0]
        p_t, e_t = {}, {}
        tr_done = {}
        ptbank_free = {2: (), 3: (), 4: ()}
        pt_t = {}
        o_free = [()]
        opair_free = [None]
        otmp_free = [None]
        ot_t, o_t, oj_t = {}, {}, {}

        def scores(h, qb):
            u, j = divmod(h, 4)
            kk = sn[0] % 2
            sn[0] += 1
            ps = bank[kk]
            n = max(256, (qb + 1) * 128)
            lhs = QT[:, u % 2, j, qb * 128:(qb + 1) * 128]
            need = [qt_t[u, qb]] + [kt_t[u, i] for i in range(n // 128)]
            pe.quiet(do_matmul(ps[:, 0:n], lhs, KT[:, u % 2, 0, 0:n], start=True, stop=False), *need, *sfree[kk])
            p = s_done[h] = pe(do_matmul(ps[:, 0:n], lhs, KT[:, u % 2, 1, 0:n], start=False, stop=True))
            n = (qb + 1) * 128
            z = h % 3
            pq = P[:, z, off[qb]:off[qb] + n]
            a = dve(do_tensor_tensor_reduce(pq, ps[:, 0:n], mask[:, 512 - n:512], -0.125, BIG, ALU.add, ALU.min,
                                            mn[:, z, qb:qb + 1]), p, t_tab, tr_done.get(h - 3))
            sfree[kk] = (a,)

            def exp():
                e_t[h, qb] = act(do_activation(pq, pq, ACT.Exp, bias=mn[:, z, qb:qb + 1], scale=-1.0,
                                               accum_out=rs[:, z, qb:qb + 1]), a)
            return exp

        def norm_p(h):
            z = h % 3
            r = dve(do_reciprocal(ri[:, z, :], rs[:, z, :]), *(e_t[h, qb] for qb in range(4)))
            for qb in range(4):
                n = (qb + 1) * 128
                pq = P[:, z, off[qb]:off[qb] + n]
                p_t[h, qb] = pool(do_tensor_tensor(pq, pq, ri[:, z, qb:qb + 1].to_broadcast([128, n]), ALU.mult), r)

        def turn_p(h, part):
            z = h % 3
            k = 2 + part
            ps = bank[k]
            todo = [[(0, qb) for qb in range(4)], [(1, 1), (1, 2), (1, 3), (3, 3)], [(2, 2), (2, 3)]][part]
            w = [p_t[h, qb] for _, qb in todo] + [*ptbank_free[k], t_c]
            for m, (kb, qb) in enumerate(todo):
                src = P[:, z, off[qb] + kb * 128:off[qb] + (kb + 1) * 128]
                (pe if m == len(todo) - 1 else pe.quiet)(
                    do_transpose(ps[:, m * 128:(m + 1) * 128], src, ident[:, :]), *w)
                w = []
            p = pe.last()
            tr_done[h] = p
            free = pv_done.get(h - 1)
            v = ps[:, 0:128 * len(todo)].rearrange("p (m n) -> p m n", n=128)
            hi = act(do_activation(pt_part(PTh, part), v, ACT.Copy), p, free)

            def rest():
                lo = dve(do_tensor_tensor(pt_part(PTl, part), v, pt_part(PTh, part).bitcast(F32), ALU.subtract), hi, free)
                ptbank_free[k] = pt_t[h, part] = (hi, lo)
            return rest

        def weigh(h):
            u, j = divmod(h, 4)
            ps = bank[5]
            need = [x for pt in range(3) for x in pt_t[h, pt]] + [x for i in range(4) for x in v_t[u, i]] + [t_z]
            w = [*need, *o_free[0]]
            seq = [(kb, T) for kb in range(4) for T in (PTh, PTl)]
            for m, (kb, T) in enumerate(seq):
                q0 = min(kb * 128, 256)
                lhs = VS[:, u % 3, kb, :, :].rearrange("p a d -> p (a d)")
                last = m == 7
                (pe if last else pe.quiet)(
                    do_matmul(ps[:, q0:512], lhs, pt_of(T, kb), start=m == 0, stop=last), *w)
                w = []
            p = pv_done[h] = pe.last()
            o_t[h] = act(do_activation(Otmp[:, :], ps[64:128, :], ACT.Copy), p, otmp_free[0])

        def join(h):
            u, j = divmod(h, 4)
            ps, a = bank[5], o_t[h]
            half = slice(64 * (j % 2), 64 * (j % 2) + 64)
            b = dve(do_tensor_tensor(Opair[half, :], ps[0:64, :], Otmp[:, :], ALU.add), a, opair_free[0])
            otmp_free[0] = b
            o_free[0] = (a, b)
            oj_t[h] = b

        wo_done = {}

        def ot_at(u, c):
            return 2 if c else u % 2

        def pair(h):
            u, j = divmod(h, 4)
            if j % 2:
                c, b = ot_at(u, j // 2), oj_t[h]
                free = wo_done.get((u - (1 if j == 3 else 2), 3))
                hh = act(do_activation(OTh[:, c, :], Opair[:, :], ACT.Copy), b, free)
                l = pool(do_tensor_tensor(OTl[:, c, :], Opair[:, :], OTh[:, c, :].bitcast(F32), ALU.subtract), hh, free)
                opair_free[0] = l
                ot_t[u, j // 2] = (hh, l)

        x_t = {}

        def attn_out(u, i, late_out):
            g, b = units[u]
            t = b * TB + i
            k = 7 if late_out else 5
            ps = bank[k]
            w = [*wo_t[g][0:2], *ot_t[u, 0], *ot_t[u, 1], *(bank_free[7] if late_out else o_free[0])]
            for c in range(2):
                if c:
                    w = wo_t[g][2:4]
                oh, ol = (T[:, ot_at(u, c), i * 128:(i + 1) * 128] for T in (OTh, OTl))
                for n, (l, r) in enumerate(((oh, Oh), (oh, Ol), (ol, Oh))):
                    last = c == 1 and n == 2
                    (pe if last else pe.quiet)(
                        do_matmul(ps[:, :], l, r[:, c, :], start=c == 0 and n == 0, stop=last), *w)
                    w = []
            p = wo_last[0] = wo_done[u, i] = pe.last()
            x_t[t] = dve(do_tensor_tensor(X[:, t, :], X[:, t, :], ps[:, :], ALU.add), p, x_t.get(t))
            if late_out:
                bank_free[7] = (x_t[t],)
            else:
                o_free[0] = (x_t[t],)

        tiles = [(u, i) for u in range(len(units)) for i in range(TB)]
        nh = 4 * len(units)

        def tile_at(n):
            return tiles[n] if 0 <= n < len(tiles) else None

        def step(h, between=None):
            new, rot, trn = tile_at(h + 6), tile_at(h + 5), tile_at(h + 4)
            wo_u, wo_m = divmod(h - 7, 4)
            wo_now = 0 <= wo_u < len(units)
            first_q = new and new[0] and new[1] == 0 and units[new[0]][1] == 0
            first_o = wo_now and wo_u and wo_m == 0 and units[wo_u][1] == 0

            def next_w(stage):
                if first_q:
                    next_wq(units[new[0]][0], stage)
                if first_o:
                    next_wo(units[wo_u][0], stage)

            next_w(0)
            if 1 <= h <= nh:
                norm_p(h - 1)
            if rot:
                value_hi(*rot)
            if 0 <= h < nh:
                scores(h, 3)()
                exp2 = scores(h, 2)
            if trn:
                turn(*trn, False)
            if 0 <= h < nh:
                exp2()
            if 3 <= h < nh + 3:
                weigh(h - 3)
            if rot:
                rotate(*rot)
            if between:
                between()
            back = 2 <= h < nh + 2
            if back:
                lo0 = turn_p(h - 2, 0)
            next_w(1)
            if 0 <= h < nh:
                scores(h, 1)()
            if 3 <= h < nh + 3:
                join(h - 3)
            if back:
                lo0()
                lo1 = turn_p(h - 2, 1)
            next_w(2)
            if trn:
                turn(*trn, True)
            if 0 <= h < nh:
                scores(h, 0)()
            if back:
                lo2 = turn_p(h - 2, 2)
                lo1()
            if rot:
                hh = parts_qk(*rot)
            if back:
                lo2()
            if rot:
                parts_qk2(*rot, *hh)
            if new:
                project(*new)
            if wo_now:
                attn_out(wo_u, wo_m, h >= nh - 4)
            if 3 <= h < nh + 3:
                pair(h - 3)



        phase.close()
        phase = root.enter_context(ExitStack())
        scope[-1] = phase
        NP = 17
        UP = 11
        U32 = mybir.dt.uint32
        NR = 6
        work = sb("work", [128, 8, 512])
        RW = sb("RW", [128, NR, 512])
        hm = sb("hm", [128, 2, 256])
        Gh = sb("Gh", [128, 4, 128], F32R)
        Gl = sb("Gl", [128, 4, 128], F32R)
        XN = sb("XN", [128, TB, D])
        Uh = sb("Uh", [128, UP, 4, 128], F32R)
        Ul = sb("Ul", [128, UP, 4, 128], F32R)
        Dh = sb("Dh", [128, 6, 512], F32R)
        Dl = sb("Dl", [128, 6, 512], F32R)
        CTh, CTl = XT[0][:, 0, :, :], XT[0][:, 1, :, :]
        YTh, YTl = ([XT[2 + z][:, n, :, :] for z in range(2)] for n in range(2))
        CW = [work[:, k, :] for k in range(3)]
        T1 = [work[:, 3 + k, :] for k in range(3)]
        T2 = [work[:, 6 + k, :] for k in range(2)]
        Hh = sb("Hh", [128, 6, 256], F32R)
        Hl = sb("Hl", [128, 5, 256], F32R)
        LG = sb("LG", [128, 512])
        Graw = sb("Graw", [128, 4, 8])
        rank = sb("rank", [128, 8])
        tri = sb("tri", [128, 128])
        trib = sb("trib", [128, 128], BF16)
        oneb = sb("oneb", [128, 128], BF16)
        lg = sb("lg", [128, 32])
        le = sb("le", [128, NT * 8])
        lq = sb("lq", [128, 32])
        lp = sb("lp", [128, 32])
        ohb = sb("ohb", [128, 32], BF16)
        cum = sb("cum", [128, 5, 8], BF16)
        sm = sb("sm", [128, 4, 4])
        kp = sb("kp", [128, NT])
        gk = sb("gk", [128, NT])
        gs = sb("gs", [128, NT])
        sidx = sb("sidx", [128, NT], U32)
        gidx = sb("gidx", [128, NT], U32)
        xd = nc.dram_tensor("xd", (NE * CAP, D), F32).ap()
        oe = nc.dram_tensor("oe", (NE * CAP, D), F32).ap()

        s_r = [slot(f"s_r{i}") for i in range(NR)]
        s_k, s_cw = slot("s_k"), [slot(f"s_cw{i}") for i in range(3)]
        s_z, s_sc = slot("s_z"), slot("s_sc")
        s_xe = [slot("s_xe0"), slot("s_xe1")]
        s_oe = [slot("s_oe0"), slot("s_oe1")]
        s_g = [slot(f"s_g{i}") for i in range(10)]
        s_o = slot("s_o")
        bf = [()] * 8
        late = {}

        def product(ps, pairs, waits, start=True, stop=True):
            w = list(waits)
            for m, (l, r) in enumerate(pairs):
                f = pe if m == len(pairs) - 1 else pe.quiet
                f(do_matmul(ps, l, r, start=start and m == 0, stop=stop and m == len(pairs) - 1), *w)
                w = []
            return pe.last()

        def three(lh, ll, rh, rl):
            return [(lh, rh), (lh, rl), (ll, rh)]

        piece_t = {}
        raw_t = {}
        piece_free = {}
        ring = [0]
        ring_free = [()] * NR
        order = [(m, p) for m in range(NE + 2) for p in range(NP)]

        def load_next():
            if ring[0] < len(order):
                m, p = order[ring[0]]
                k = ring[0] % NR
                raw_t[m, p] = (k, sp.dma(do_dma_start(RW[:, k, :], wf_in[m % (NE + 1), p]), s_r[k], *(ring_free[k] or late["w"])))
                ring[0] += 1

        def split_piece(m, p):
            k, t = raw_t[m, p]
            if p < UP:
                h, l = Uh[:, p, :, :].rearrange("p c n -> p (c n)"), Ul[:, p, :, :].rearrange("p c n -> p (c n)")
            else:
                h, l = Dh[:, p - UP, :], Dl[:, p - UP, :]
            free = [piece_free[p]] if p in piece_free else late["x" if p < UP else "all"]
            a = act(do_activation(h, RW[:, k, :], ACT.Copy), t, *free)
            b = (pool if p % 2 else dve)(do_tensor_tensor(l, RW[:, k, :], h.bitcast(F32), ALU.subtract), a, *free)
            piece_t[m, p] = (a, b)
            ring_free[k] = (b,)
            load_next()

        c_t, z_n = {}, []

        def zero_rows():
            xdz = xd.rearrange("(t p) d -> t p d", p=128)
            if not z_n:
                c_t["z"] = pool(do_memset(T1[0], 0.0), late["work"])
            for t in range(len(z_n), len(z_n) + 2):
                z_n.append(t)
                c_t["zero"] = t1_free[0] = sp.dma(do_dma_start(xdz[t], T1[0]), s_z, c_t["z"])

        def constants():
            w = late["all"]
            t_k = [sp.dma(do_dma_start(d, v), s_k, *w)
                   for d, v in ((Graw[:, :, :], wg_in), (rank[:, :], rank_in), (tri[:, :], tri_in))][-1]
            z = pool(do_memset(Gh[:, :, :].bitcast(F32), 0.0), *w)
            z1 = pool(do_memset(Gl[:, :, :].bitcast(F32), 0.0))
            c_t["one"] = pool(do_memset(oneb[:, :], 1.0))
            run_t[0] = pool(do_memset(cum[:, 0, :], 0.0))
            h = act(do_activation(Gh[:, :, 0:8], Graw[:, :, :], ACT.Copy), t_k, z)
            l = pool(do_tensor_tensor(Gl[:, :, 0:8], Graw[:, :, :], Gh[:, :, 0:8].bitcast(F32), ALU.subtract), h, z1)
            c_t["g"] = (h, l)
            c_t["tri"] = act(do_activation(trib[:, :], tri[:, :], ACT.Copy), t_k)
            c_t["rank"] = t_k

        cv = ctx_in.rearrange("(b i p) d -> b i p d", p=128, i=TB)
        cw_n, cw_free, cw_at = [0], [None] * 3, {}

        def load_cw(b, i, n):
            k = cw_n[0] % 3
            cw_n[0] += 1
            cw_at[b, i, n] = (k, sp.dma(do_dma_start(CW[k], cv[b, i]), s_cw[k], cw_free[k] or late["work"]))

        t2_n, t2_free = [0], [None, None]

        def scales(amax, r, d, least, *waits):
            a = dve(do_tensor_scalar(d, amax, least, None, ALU.max), *waits)
            a = dve(do_reciprocal(r, d), a)
            a = dve(do_tensor_scalar(r, r, 448.0, None, ALU.mult), a)
            return dve(do_tensor_scalar(d, d, 1.0 / 448.0, None, ALU.mult), a)

        def blocks(y):
            return y.rearrange("p (c n) -> p c n", c=4)

        def rounded(engine, y, r, d, *waits):
            k = t2_n[0] % 2
            t2_n[0] += 1
            q = T2[k]
            a = dve(do_tensor_tensor(blocks(y), blocks(y), r.unsqueeze(2).to_broadcast([128, 4, 128]), ALU.mult), *waits)
            a = dve(do_tensor_scalar(q.bitcast(U32), y.bitcast(U32), 0x7F800000, None, ALU.bitwise_and), a,
                    t2_free[k] or late["work"])
            a = dve(do_tensor_scalar(q, q, 2.0 ** -6, 1.5 * 2.0 ** 20, ALU.max, ALU.mult), a)
            a = engine(do_tensor_tensor(y, y, q, ALU.add), a)
            a = t2_free[k] = engine(do_tensor_tensor(y, y, q, ALU.subtract), a)
            return pool(do_tensor_tensor(blocks(y), blocks(y), d.unsqueeze(2).to_broadcast([128, 4, 128]), ALU.mult), a)

        tb, tbanks = [0], [(6,)]

        def turned(engine, src, dh, dl, wait, *free):
            k = tbanks[0][tb[0] % len(tbanks[0])]
            tb[0] += 1
            p = transposed(src, bank[k], wait, *bf[k])
            ps = bank[k][:, :].rearrange("p (c n) -> p c n", c=4)
            h = act(do_activation(dh, ps, ACT.Copy), p, *free)

            def rest():
                l = engine(do_tensor_tensor(dl, ps, dh.bitcast(F32), ALU.subtract), h, *free)
                bf[k] = (h, l)
                return h, l
            return p, rest

        ct_t, ct_free = {}, [None]
        k_t = {}

        def context_max(b, i):
            k, t = cw_at[b, i, 0]
            k_t[b, i] = cw_free[k] = dve(do_tensor_reduce(
                wam[:, i, :], CW[k].rearrange("p (c n) -> p c n", c=4), AX.X, ALU.max, apply_absolute_value=True), t)

        def context_all(b):
            k_t[b] = pool(do_partition_all_reduce(wsc[:, 0, :], wam[:, :, :].rearrange("p i c -> p (i c)"), 128,
                                                  bass.bass_isa.ReduceOp.max), *(k_t[b, i] for i in range(TB)), ct_free[0])

        def context_scales(b):
            k_t[b] = scales(wsc[:, 0, :], wsc[:, 1, :], wsc[:, 0, :], 1e-6, k_t[b])

        def context_round(b, i):
            k, t = cw_at[b, i, 1]
            k_t[b, i] = rounded(pool, CW[k], wsc[:, 1, 4 * i:4 * i + 4], wsc[:, 0, 4 * i:4 * i + 4], t, k_t[b])

        def context_turn(b, i):
            k, _ = cw_at[b, i, 1]
            sl = slice(i * 128, (i + 1) * 128)
            cw_free[k], rest = turned(dve, CW[k], CTh[:, :, sl], CTl[:, :, sl], k_t[b, i], ct_free[0])

            def end():
                ct_t[b, i] = rest()
            return end

        t1_free = [None] * 3
        yt_free = [None, None]
        q_t, x2_t, y_t, n2_t, n3_t = {}, {}, {}, {}, {}

        def stats2(b, i):
            n2_t[b] = stats_of(b * TB + i, x_t[b * TB + i])

        def norm2(b):
            n2_t[b] = rstd_of(slice(b * TB, (b + 1) * TB), n2_t[b])

        def cross_round(b, i):
            t = b * TB + i
            y = T1[t % 3]
            a = normed(y, t, n2_t[b], t1_free[t % 3] or late["work"])
            a = dve(do_tensor_reduce(aam[:, i, :], blocks(y), AX.X, ALU.max, apply_absolute_value=True), a)
            a = scales(aam[:, i, :], asc[:, i, 0, :], asc[:, i, 1, :], 1e-4, a)
            q_t[t] = rounded(pool, y, asc[:, i, 0, :], asc[:, i, 1, :], a)

        def cross_turn(b, i):
            t, z = b * TB + i, b % 2
            sl = slice(i * 128, (i + 1) * 128)
            t1_free[t % 3], rest = turned(dve, T1[t % 3], YTh[z][:, :, sl], YTl[z][:, :, sl], q_t[t], yt_free[z])

            def end():
                q_t[t] = rest()
            return end

        def cross_product(b, i):
            t, z = b * TB + i, b % 2
            sl = slice(i * 128, (i + 1) * 128)
            pairs = [x for c in range(4) for x in three(YTh[z][:, c, sl], YTl[z][:, c, sl], CTh[:, c, :], CTl[:, c, :])]
            p = product(bank[6][:, :], pairs, [*q_t[t], *(x for q in range(TB) for x in ct_t[b, q]), *bf[6]])
            y_t[t] = ct_free[0] = p

            def end():
                x2_t[t] = dve(do_tensor_tensor(X[:, t, :], X[:, t, :], bank[6][:, :], ALU.add), p)
                bf[6] = (x2_t[t],)
                n3_t[b * TB + i] = stats_of(t, x2_t[t])
            return end

        run_t = [None]
        scat = [None]
        ready_y = {}
        lg_t, lg_free = {}, [None]
        small_free = [None]
        mx, em, ps_, fl = (sm[:, j, :] for j in range(4))
        l3, q3, p3 = (v[:, :].rearrange("p (i e) -> p i e", e=8) for v in (lg, lq, lp))

        def wide(v):
            return v.unsqueeze(2).to_broadcast([128, 4, 8])

        def rstd3(b):
            n3_t[b, 0] = rstd_of(slice(b * TB, (b + 1) * TB), *(n3_t[b * TB + i] for i in range(TB)))

        def norm3(b, i):
            t = b * TB + i
            n3_t[t] = normed(XN[:, i, :], t, n3_t[b, 0], *([scat[0]] if scat[0] else late["x"]))

        def route_turn(b, i):
            t, z = b * TB + i, b % 2
            sl = slice(i * 128, (i + 1) * 128)
            _, rest = turned(dve, XN[:, i, :], YTh[z][:, :, sl], YTl[z][:, :, sl], n3_t[t], y_t[t])

            def end():
                ready_y.setdefault(b, []).extend(rest())
            return end

        def logits(b):
            z = b % 2
            pairs = [x for c in range(4) for x in three(Gh[:, c, :], Gl[:, c, :], YTh[z][:, c, :], YTl[z][:, c, :])]
            p = product(bank[6][:, :], pairs, [*c_t["g"], *ready_y[b], *bf[6]])
            a = act(do_activation(LG[:, :], bank[6][:, :], ACT.Copy), p, lg_free[0], *late["all"])
            bf[6] = (a,)
            lg_t[b] = a

        def choose(b):
            a = lg_t[b]
            k = tbanks[0][tb[0] % len(tbanks[0])]
            tb[0] += 1
            lg_free[0] = p = transposed(LG, bank[k], a, *bf[k])
            e3 = le[:, b * 32:b * 32 + 32].rearrange("p (i e) -> p i e", e=8)
            rk = rank[:, :].unsqueeze(1).to_broadcast([128, 4, 8])
            a = dve(do_tensor_copy(l3, bank[k][:, :].rearrange("p (i n) -> p i n", i=4)[:, :, 0:8]), p, small_free[0])
            bf[k] = (a,)
            m = dve(do_tensor_reduce(mx, l3, AX.X, ALU.max), a)
            d = dve(do_tensor_tensor(e3, l3, wide(mx), ALU.subtract), m)
            q = dve(do_tensor_tensor(q3, l3, wide(mx), ALU.is_equal), m)
            q = dve(do_tensor_tensor(q3, q3, rk, ALU.mult), q, c_t["rank"])
            q = dve(do_tensor_reduce(em, q3, AX.X, ALU.min), q)
            oh = dve(do_tensor_tensor(q3, rk, wide(em), ALU.is_equal), q)
            ob = dve(do_tensor_copy(ohb[:, :], lq[:, :]), oh)
            r = run_t[0]
            for i in range(TB):
                r = dve(do_tensor_tensor(cum[:, i + 1, :], cum[:, i, :], lq[:, i * 8:(i + 1) * 8], ALU.add), oh, r)
            lg_t[b] = (d, ob, r)

        def place(b):
            ts = slice(b * TB, (b + 1) * TB)
            d, ob, r = lg_t[b]
            p = product(bank[6][:, 0:32], [(trib[:, :], ohb[:, :]), (oneb[:, :], cum[:, 0:4, :].rearrange("p i e -> p (i e)"))],
                        [ob, r, c_t["tri"], c_t["one"], *bf[6]])
            run_t[0] = dve(do_tensor_copy(cum[:, 0, :], cum[:, 4, :]), p, r)
            v = dve(do_tensor_tensor(p3, bank[6][:, 0:32].rearrange("p (i e) -> p i e", e=8), q3, ALU.mult), p)
            bf[6] = (v,)
            v = dve(do_tensor_reduce(ps_, p3, AX.X, ALU.add), v)
            h = dve(do_tensor_scalar(kp[:, ts], ps_, float(CAP), None, ALU.is_lt), v)
            v = dve(do_scalar_tensor_tensor(fl, em, float(CAP), ps_, ALU.mult, ALU.add), v)
            v = dve(do_tensor_scalar(fl, fl, 1.0, float(8 * CAP + 4096), ALU.mult, ALU.add), v)
            v = dve(do_scalar_tensor_tensor(fl, kp[:, ts], -4096.0, fl, ALU.mult, ALU.add), v, h)
            v1 = dve(do_tensor_copy(sidx[:, ts], fl), v)
            v2 = dve(do_tensor_scalar(gidx[:, ts], fl, float(NE * CAP - 1), None, ALU.min), v)
            small_free[0] = v2
            for i in range(TB):
                t = b * TB + i
                scat[0] = pool.dma(do_indirect_dma_start(
                    xd, bass.IndirectOffsetOnAxis(ap=sidx[:, t:t + 1], axis=0), XN[:, i, :], None,
                    bounds_check=NE * CAP - 1, oob_is_err=False), s_sc, v1, c_t["zero"])

        def gates():
            e3 = le[:, :].rearrange("p (t e) -> p t e", e=8)
            a = act(do_activation(le[:, :], le[:, :], ACT.Exp), dve.last())
            a = dve(do_tensor_reduce(gs[:, :], e3, AX.X, ALU.add), a)
            a = dve(do_reciprocal(gk[:, :], gs[:, :]), a)
            return dve(do_tensor_tensor(gk[:, :], gk[:, :], kp[:, :], ALU.mult), a)

        h_free = [()]
        hn = [0]
        hm_free = [None, None]
        MAIN = -5
        up_n = [0]

        def expert(m, yh, yl, ready, done, split_next):
            def piece(p):
                if split_next and m <= NE:
                    split_piece(m + 1, p)

            ht = [[] for _ in range(6)]

            def parts(c, s, d):
                if c < 5:
                    h = act(do_activation(Hh[:, c, :], hm[:, s, :], ACT.Copy), d, *h_free[0])
                    l = dve(do_tensor_tensor(Hl[:, c, :], hm[:, s, :], Hh[:, c, :].bitcast(F32), ALU.subtract), h, *h_free[0])
                else:
                    h = act(do_activation(Hh[0:64, 5, :], hm[0:64, s, :], ACT.Copy), d, *h_free[0])
                    l = dve(do_tensor_tensor(Hh[64:128, 5, :], hm[0:64, s, :], Hh[0:64, 5, :].bitcast(F32), ALU.subtract),
                            h, *h_free[0])
                hm_free[s] = l
                ht[c] = [h, l]

            prev = None
            for c in range(6):
                k = (4, 5, 7)[up_n[0] % 3]
                up_n[0] += 1
                ps = bank[k]
                for n, q in enumerate((2 * c, 2 * c + 1) if c < 5 else (10,)):
                    pairs = [x for kc in range(4) for x in three(Uh[:, q, kc, :], Ul[:, q, kc, :], yh(kc), yl(kc))]
                    p = product(ps[:, 256 * n:256 * n + 256], pairs, [*ready, *piece_t[m, q], *bf[k]])
                    piece_free[q] = p
                if prev:
                    parts(*prev)
                s = hn[0] % 2
                hn[0] += 1
                if c < 5:
                    a = act(do_activation(hm[:, s, :], ps[:, 0:256], ACT.Silu), p, hm_free[s])
                    d = dve(do_tensor_tensor(hm[:, s, :], hm[:, s, :], ps[:, 256:512], ALU.mult), a, p)
                else:
                    a = act(do_activation(hm[0:64, s, :], ps[0:64, 0:256], ACT.Silu), p, hm_free[s])
                    d = dve(do_tensor_tensor(hm[0:64, s, :], hm[0:64, s, :], ps[64:128, 0:256], ALU.mult), a, p)
                bf[k] = (a, d)
                prev = (c, s, d)
                if c:
                    piece(2 * c - 2)
                    piece(2 * c - 1)
                yield
            parts(*prev)
            piece(10)
            dt = [x for q in range(UP, NP) for x in piece_t[m, q]]
            for i in range(2):
                sl = slice(i * 128, (i + 1) * 128)
                for c in range(5):
                    product(bank[2 + i][:, :], three(Hh[:, c, sl], Hl[:, c, sl], Dh[:, c, :], Dl[:, c, :]),
                            [*ht[c], *(dt if not c else ()), *(bf[2 + i] if not c else ())], start=not c, stop=False)
            yield
            for i in range(2):
                sl = slice(i * 128, (i + 1) * 128)
                p = product(bank[2 + i][:, :], [(Hh[:, 5, sl], Dh[:, 5, :]), (Hh[:, 5, sl], Dl[:, 5, :])], ht[5], start=False)
                bf[2 + i] = (done(i, 2 + i, p),)
            h_free[0] = (p,)
            for q in range(UP, NP):
                piece_free[q] = p
            for q in range(UP, NP):
                piece(q)
            yield

        def shared(m, b, half, split_next, last=None):
            z = b % 2
            o = half * 256

            def done(i, k, p):
                t = b * TB + 2 * half + i
                x2_t[t] = dve(do_tensor_tensor(X[:, t, :], X[:, t, :], bank[k][:, :], ALU.add), p, x2_t[t])
                if last:
                    last(t)
                return x2_t[t]

            yield from expert(m, lambda kc: YTh[z][:, kc, o:o + 256], lambda kc: YTl[z][:, kc, o:o + 256], ready_y[b], done,
                              split_next)
            yt_free[z] = pe.last()

        xe_t, xt_e = {}, {}
        XE = XN[:, :, :].rearrange("p (z i) d -> p z i d", z=2)
        xdv = xd.rearrange("(m i p) d -> m p i d", p=128, i=2)
        oev = oe.rearrange("(m i p) d -> m i p d", p=128, i=2)
        xe_free = [None, None]

        def load_x(m):
            xe_t[m] = sp.dma(do_dma_start(XE[:, m % 2, :, :], xdv[m]), s_xe[m % 2], xe_free[m % 2], scat[0])

        def turn_x(m, i):
            z = m % 2
            sl = slice(i * 128, (i + 1) * 128)
            xe_free[z], rest = turned(dve, XE[:, z, i, :], YTh[z][:, :, sl], YTl[z][:, :, sl], xe_t[m], yt_free[z])
            xt_e.setdefault(m, []).extend(rest())

        side = {}

        def plan(s, f, *a):
            side.setdefault(s, []).append((f, a))

        def plan_context(b, s):
            def first(i):
                context_max(b, i)
                load_cw(b, *((3, 0) if i == 0 else (i - 1, 1)))

            def turn_and_load(i):
                end = context_turn(b, i)
                if i == 0:
                    load_cw(b, 3, 1)
                elif b + 1 < NB:
                    load_cw(b + 1, i - 1, 0)
                return end

            for i in range(TB):
                plan(s + i // 2, first, i)
            plan(s + 2, context_all, b)
            plan(s + 3, context_scales, b)
            for i in range(TB):
                at = s + 4 + i + i // 3
                plan(at, context_round, b, i)
                plan(at + 2, turn_and_load, i)

        def plan_cross(b, s):
            for i in range(TB):
                plan(s - 13 + i if b else s - 3 + i // 2, stats2, b, i)
                plan(s + 1 + i, cross_turn, b, i)
                plan(s + 2 + i, cross_product, b, i)
                plan(s - 1 + i, cross_round, b, i)
                plan(s + 7 + i // 2, norm3, b, i)
                plan(s + 9 + i // 2, route_turn, b, i)
            plan(s - (7 if b else 2), norm2, b)
            plan(s + 6, rstd3, b)
            plan(s + 12, logits, b)
            plan(s + 14, choose, b)
            plan(s + (19 if b < NB - 1 else 15), place, b)

        for b in range(NB):
            plan_cross(b, 16 * (b - 1))
            plan_context(b, 16 * (b - 1) - 10)

        kinds = [route_turn, cross_turn, logits, choose, place, cross_product]

        for i in range(2):
            plan(16 * NB - 16, load_x, i)
            plan(16 * NB - 14 + i, turn_x, 0, i)

        def run_slot(s):
            fs = side.pop(s, [])
            fs.sort(key=lambda fa: kinds.index(fa[0]) if fa[0] in kinds else len(kinds) - (fa[0].__name__ == "turn_and_load") * 9)
            for g in [g for g in [f(*a) for f, a in fs] if g]:
                g()

        def side_slot():
            run_slot(slot_n[0])
            slot_n[0] += 1

        pieces = list(range(NP))

        def split_first(n):
            for _ in range(min(n, len(pieces))):
                split_piece(0, pieces.pop(0))

        slot_n = [-26]
        for h in range(-6, nh + 7):
            if h == 0:
                tr_done.update({m: xn_free[5] for m in (-3, -2, -1)})
                sfree[:] = bank_free[0:2]
                ptbank_free.update({2: bank_free[2], 3: bank_free[3]})
                wo_t[0] = split_w(Oraw, Oh, Ol, t_wo[0], (pool, dve))
            if h == 1:
                ptbank_free[4] = bank_free[4]
            if h == 8:
                load_wq(1, *wo_t[0], xn_free[6])
            step(h, side_slot if h >= nh - 11 else None)
            if TB <= h + 8 < NT:
                o_free[0] = first_turn(h + 8, 5, o_free[0])
            if h == -5:
                first_rstd(1, 2)
            if -5 <= h < -1:
                first_stats(2 * h + 18)
                first_stats(2 * h + 19)
            if h == -2:
                first_rstd(2, 4)
            if TB <= h + 9 < NT:
                first_norm(h + 9)
            if h == nh - 19:
                ct_free[0] = proj_last[0]
            if h == nh - 14:
                late["work"] = proj_last[0]
                for i in range(3):
                    load_cw(0, i, 0)
            if nh - 12 <= h < nh - 4:
                zero_rows()
            if h == nh - 11:
                yt_free[0] = proj_last[0]
            if h == nh - 6:
                yt_free[1] = proj_last[0]
                bf[6] = bank_free[6]
                late["w"] = (proj_last[0], *wo_t[NG - 1])
                for _ in range(NR):
                    load_next()
            if h == nh - 1:
                bf[0], bf[1] = sfree
                tbanks[0] = (0, 1)
            if h == nh + 2:
                late["x"] = [x.last() for x in (pe, act, dve, pool)]
            if h > nh + 2:
                split_first(2)
        late["all"] = [x.last() for x in (pe, act, dve, pool)]
        h_free[0] = tuple(late["all"])
        for k in (2, 3, 4, 5, 7):
            bf[k] = tuple(late["all"])
        constants()
        while slot_n[0] < MAIN:
            side_slot()
            split_first(4)
        split_first(NP)
        for n in range(2 * NB - 1):
            b, half = divmod(n, 2)
            chunks = shared(0, b, half, n == 2 * NB - 2)
            for _ in range(8):
                side_slot()
                next(chunks)
            for _ in chunks:
                pass
        while side:
            side_slot()

        OE = T2
        oe_free = list(t2_free)
        t_gk = gates()
        for m in range(NE):
            z = m % 2

            def done(i, k, p):
                r = act(do_activation(OE[i], bank[k][:, :], ACT.Copy), p, oe_free[i])
                oe_free[i] = sp.dma(do_dma_start(oev[m, i], OE[i]), s_oe[i], r)
                return r

            for n, _ in enumerate(expert(m + 1, lambda kc: YTh[z][:, kc, 0:256], lambda kc: YTl[z][:, kc, 0:256],
                                         xt_e[m], done, True)):
                if n in (1, 2) and m + 1 < NE:
                    turn_x(m + 1, n - 1)
                if n == 2 and m + 2 < NE:
                    load_x(m + 2)
            yt_free[z] = pe.last()

        G = [XN[:, k, :] for k in range(TB)] + CW + T1
        ov = out.rearrange("(t p) d -> t p d", p=128)
        g_free = [(xe_free[0], xe_free[1], *cw_free, *t1_free)] * len(G)
        g_t = {}

        def gather(t):
            k = t % len(G)
            g_t[t] = pool.dma(do_indirect_dma_start(G[k], None, oe, bass.IndirectOffsetOnAxis(ap=gidx[:, t:t + 1], axis=0)),
                              s_g[k], *oe_free, *g_free[k])

        def store(t):
            sp.dma(do_dma_start(ov[t], X[:, t, :]), s_o, x2_t[t])

        def combine(t):
            k = t % len(G)
            x2_t[t] = dve(do_scalar_tensor_tensor(X[:, t, :], G[k], gk[:, t:t + 1], X[:, t, :], ALU.mult, ALU.add),
                          g_t[t], x2_t[t], t_gk)
            g_free[k] = (x2_t[t],)
            if t < NT - 2:
                store(t)

        tg = list(range(NT))
        for t in range(len(G)):
            gather(t)
        for n, _ in enumerate(shared(NE + 1, NB - 1, 1, False, store)):
            for _ in range((0, 1, 2, 3, 3, 3, 4)[n] if n < 7 else 0):
                if tg:
                    t = tg.pop(0)
                    combine(t)
                    if t + len(G) < NT:
                        gather(t + len(G))
        sp.wait((s_o[0], s_o[1]))

        with nc.Block() as block:
            block.tensor(pe.emit)
            block.scalar(act.emit)
            block.vector(dve.emit)
            block.gpsimd(pool.emit)
            block.sync(sp.emit)


def kernel(**inputs):
    import concourse.bacc as bacc
    from concourse import mybir as mb
    from concourse.bass_utils import run_bass_kernel_spmd as run

    f = np.float32
    a = {k: np.asarray(v) for k, v in inputs.items()}
    pos = np.arange(512, dtype=f)
    freq = (10000.0 ** (-np.arange(0, 64, 2, dtype=np.float64) / 64)).astype(f)
    theta = np.outer(pos, freq).astype(f).astype(np.float64)
    c, s = np.cos(theta).astype(f), np.sin(theta).astype(f)
    tab = lambda m: np.ascontiguousarray(m.reshape(4, 128, 64).transpose(1, 0, 2))
    mask = np.zeros((128, 512), f)
    mask[:, 384:] = np.where(np.arange(128)[None, :] > np.arange(128)[:, None], f(-BIG), f(0))
    kc = lambda w: np.ascontiguousarray(w.reshape(w.shape[0] // 128, 128, w.shape[1]).transpose(1, 0, 2))
    wq, wk, wv, wo = (a[f"L0_attn_{n}"] for n in ("wq", "wk", "wv", "wo"))
    wqkv = np.stack([kc(np.concatenate([wq[:, 256 * g:256 * g + 256], wk[:, 64 * g:64 * g + 64],
                                        wv[:, 64 * g:64 * g + 64]], axis=1)) for g in range(NG)])
    wog = np.stack([kc(wo[256 * g:256 * g + 256]) for g in range(NG)])

    def cut(w1, w3, w2):
        cols = [w[:, 128 * n:128 * n + 128] for n in range(5) for w in (w1, w3)]
        cols.append(np.concatenate([w1[:, 640:], w3[:, 640:]], axis=1))
        rows = [w2[128 * n:128 * n + 128] for n in range(5)] + [np.concatenate([w2[640:], w2[640:]])]
        return np.stack([kc(w).reshape(128, 512) for w in cols] + rows)

    fw = [a[f"L0_ffn_{n}"] for n in ("W1", "W3", "W2")]
    pieces = np.stack([cut(*(a[f"L0_ffn_{n}"] for n in ("sw1", "sw3", "sw2")))] + [cut(*(w[m] for w in fw)) for m in range(NE)])
    arrays = {
        "x": np.ascontiguousarray(a["x"].reshape(2048, 512)),
        "ctx": np.ascontiguousarray(a["ctx_2048"].reshape(2048, 512)),
        "wqkv": wqkv, "wo": wog,
        "wg": kc(a["L0_ffn_Wg"]), "wf": pieces,
        "ident": np.eye(128, dtype=f), "mask": mask,
        "cos": tab(np.concatenate([c, c], 1)), "sin": tab(np.concatenate([-s, s], 1)),
        "rank": np.tile(np.arange(-8, 0, dtype=f), (128, 1)),
        "tri": np.triu(np.ones((128, 128), f), 1),
    }
    nc = bacc.Bacc("TRN2", target_bir_lowering=False, num_devices=1)
    args = [nc.dram_tensor(f"in_{k}", v.shape, mb.dt.float32, kind="ExternalInput").ap() for k, v in arrays.items()]
    o = nc.dram_tensor("out", (2048, 512), mb.dt.float32, kind="ExternalOutput").ap()
    decoder(nc, *args, o)
    r = run(nc, [{f"in_{k}": v for k, v in arrays.items()}], core_ids=[0])
    return r.results[0]["out"].reshape(4, 512, 512)
```
